# Optimizing a Trainium2 kernel written in Bass

```python
import numpy as np
import jax
import jax.numpy as jnp

def _softmax(x, axis=-1):
    return jax.nn.softmax(x, axis=axis)

def _gelu(x):
    return jax.nn.gelu(x, approximate=True)

def _silu(x):
    return jax.nn.silu(x)

def _sigmoid(x):
    return jax.nn.sigmoid(x)

def _layernorm(x, axis=-1, eps=1e-05):
    m = jnp.mean(x, axis=axis, keepdims=True)
    v = jnp.var(x, axis=axis, keepdims=True)
    return (x - m) / jnp.sqrt(v + eps)

def _scatter_add(tgt, idx, src, axis=0):
    return tgt.at[idx].add(src)

def _segment_sum(src, seg, n):
    return jax.ops.segment_sum(src, seg, n)
kernel_name = 'mk_xattn_ffn_d1_seqx_r4_1ac5d1'

def setup_inputs(seed: int=0):
    np.random.seed(seed)
    _w = jnp.asarray

    def _rec_inputs():
        import jax
        import jax.numpy as jnp
        _rk = jax.random.key(seed)
        x = -0.0001661 + 0.9999 * jax.random.normal(jax.random.fold_in(_rk, 1), (8, 256, 512), jnp.float32)
        _lenS = 256 - jax.random.randint(jax.random.fold_in(_rk, 7), (8,), 0, max(1, 256 // 4) + 1, jnp.int32)
        _lenS2 = 256 - jax.random.randint(jax.random.fold_in(_rk, 8), (8,), 0, max(1, 256 // 4) + 1, jnp.int32)
        _ctx_2048P = jax.random.normal(jax.random.fold_in(_rk, 11), (8, 16, 512), jnp.float32)
        _ctx_2048c = jax.random.dirichlet(jax.random.fold_in(_rk, 511), 0.3 * jnp.ones((16,), jnp.float32), (8, 256))
        _ctx_2048t = jnp.einsum('bsk,bkd->bsd', _ctx_2048c, _ctx_2048P)
        _ctx_2048t = _ctx_2048t * jax.lax.rsqrt(jnp.mean(jnp.square(_ctx_2048t)) + 1e-12) * 0.953939
        ctx_2048 = -0.00016346 + 1.00032 * (_ctx_2048t + 0.3 * jax.random.normal(jax.random.fold_in(_rk, 611), (8, 256, 512), jnp.float32))
        return (x, ctx_2048, _lenS2)
    x, ctx_2048, _lenS2 = _rec_inputs()

    def _L0_xattn_setup():
        import jax, jax.numpy as jnp
        import numpy as np
        DIM = 512
        HEADS = 16
        HEAD_DIM = DIM // HEADS
        EPS = 1e-06
        IMG_TOKENS = 257
        B, L1, L2 = (2, 1024, 769)
        SCALE = 1.0 / np.sqrt(HEAD_DIM).astype(np.float32)

        def rms_norm(x, g):
            return x * jax.lax.rsqrt(jnp.mean(x * x, axis=-1, keepdims=True) + EPS) * g

        def attention(q, k, v, kv_mask=None):
            s = jnp.einsum('bqhd,bkhd->bhqk', q, k) * SCALE
            if kv_mask is not None:
                s = jnp.where(kv_mask[:, None, None, :], s, jnp.float32(-1000000000.0))
            p = jax.nn.softmax(s, axis=-1)
            return jnp.einsum('bhqk,bkhd->bqhd', p, v)
        key = jax.random.key(seed)
        ks = jax.random.split(key, 20)
        std = 0.02

        def lin(i):
            return (jax.random.normal(ks[i], (DIM, DIM), jnp.float32) * std, jnp.zeros((DIM,), jnp.float32))
        w_q, b_q = lin(0)
        w_k, b_k = lin(1)
        w_v, b_v = lin(2)
        w_k_img, b_k_img = lin(3)
        w_v_img, b_v_img = lin(4)
        w_o, b_o = lin(5)
        return {'x': jax.random.normal(ks[6], (B, L1, DIM), jnp.float32), 'context': jax.random.normal(ks[7], (B, L2, DIM), jnp.float32), 'context_lens': jax.random.randint(ks[8], (B,), 64, 513, jnp.int64 if jax.config.jax_enable_x64 else jnp.int32), 'w_q': w_q, 'b_q': b_q, 'w_k': w_k, 'b_k': b_k, 'w_v': w_v, 'b_v': b_v, 'w_k_img': w_k_img, 'b_k_img': b_k_img, 'w_v_img': w_v_img, 'b_v_img': b_v_img, 'w_o': w_o, 'b_o': b_o, 'g_q': jnp.ones((DIM,), jnp.float32), 'g_k': jnp.ones((DIM,), jnp.float32), 'g_k_img': jnp.ones((DIM,), jnp.float32)}
    _L0_xattn_all = _L0_xattn_setup()
    _L0_xattn_in = {k: v for k, v in _L0_xattn_all.items() if k in ('w_q', 'b_q', 'w_k', 'b_k', 'w_v', 'b_v', 'w_k_img', 'b_k_img', 'w_v_img', 'b_v_img', 'w_o', 'b_o', 'g_q', 'g_k', 'g_k_img')}
    del _L0_xattn_all

    def _L0_ffn_setup():
        import jax, jax.numpy as jnp
        import numpy as np
        ALPHA = 1.702
        LIMIT = 7.0
        TOP_K = 2
        E, H, I = (8, 512, 512)
        B, S = (2, 512)
        key = jax.random.key(seed)
        ks = jax.random.split(key, 7)
        return {'hidden_states': jax.random.normal(ks[0], (B, S, H), dtype=jnp.float32), 'router_weight': jax.random.normal(ks[1], (E, H), dtype=jnp.float32) * 0.02, 'router_bias': jax.random.normal(ks[2], (E,), dtype=jnp.float32) * 0.02, 'gate_up_proj': jax.random.normal(ks[3], (E, H, 2 * I), dtype=jnp.float32) * 0.02, 'gate_up_proj_bias': jax.random.normal(ks[4], (E, 2 * I), dtype=jnp.float32) * 0.02, 'down_proj': jax.random.normal(ks[5], (E, I, H), dtype=jnp.float32) * 0.02, 'down_proj_bias': jax.random.normal(ks[6], (E, H), dtype=jnp.float32) * 0.02}
    _L0_ffn_all = _L0_ffn_setup()
    _L0_ffn_in = {k: v for k, v in _L0_ffn_all.items() if k in ('router_weight', 'router_bias', 'gate_up_proj', 'gate_up_proj_bias', 'down_proj', 'down_proj_bias')}
    del _L0_ffn_all
    return {'x': x, 'ctx_2048': ctx_2048, '_lenS2': _lenS2, 'L0_xattn_w_q': _L0_xattn_in['w_q'], 'L0_xattn_b_q': _L0_xattn_in['b_q'], 'L0_xattn_w_k': _L0_xattn_in['w_k'], 'L0_xattn_b_k': _L0_xattn_in['b_k'], 'L0_xattn_w_v': _L0_xattn_in['w_v'], 'L0_xattn_b_v': _L0_xattn_in['b_v'], 'L0_xattn_w_k_img': _L0_xattn_in['w_k_img'], 'L0_xattn_b_k_img': _L0_xattn_in['b_k_img'], 'L0_xattn_w_v_img': _L0_xattn_in['w_v_img'], 'L0_xattn_b_v_img': _L0_xattn_in['b_v_img'], 'L0_xattn_w_o': _L0_xattn_in['w_o'], 'L0_xattn_b_o': _L0_xattn_in['b_o'], 'L0_xattn_g_q': _L0_xattn_in['g_q'], 'L0_xattn_g_k': _L0_xattn_in['g_k'], 'L0_xattn_g_k_img': _L0_xattn_in['g_k_img'], 'L0_ffn_router_weight': _L0_ffn_in['router_weight'], 'L0_ffn_router_bias': _L0_ffn_in['router_bias'], 'L0_ffn_gate_up_proj': _L0_ffn_in['gate_up_proj'], 'L0_ffn_gate_up_proj_bias': _L0_ffn_in['gate_up_proj_bias'], 'L0_ffn_down_proj': _L0_ffn_in['down_proj'], 'L0_ffn_down_proj_bias': _L0_ffn_in['down_proj_bias']}

def reference(x, ctx_2048, _lenS2, L0_xattn_w_q, L0_xattn_b_q, L0_xattn_w_k, L0_xattn_b_k, L0_xattn_w_v, L0_xattn_b_v, L0_xattn_w_k_img, L0_xattn_b_k_img, L0_xattn_w_v_img, L0_xattn_b_v_img, L0_xattn_w_o, L0_xattn_b_o, L0_xattn_g_q, L0_xattn_g_k, L0_xattn_g_k_img, L0_ffn_router_weight, L0_ffn_router_bias, L0_ffn_gate_up_proj, L0_ffn_gate_up_proj_bias, L0_ffn_down_proj, L0_ffn_down_proj_bias):
    import jax
    import jax.numpy as jnp

    def _L0_xattn_ref(x, context, context_lens, w_q, b_q, w_k, b_k, w_v, b_v, w_k_img, b_k_img, w_v_img, b_v_img, w_o, b_o, g_q, g_k, g_k_img):
        import jax, jax.numpy as jnp
        import numpy as np
        DIM = 512
        HEADS = 16
        HEAD_DIM = DIM // HEADS
        EPS = 1e-06
        IMG_TOKENS = 257
        B, L1, L2 = (2, 1024, 769)
        SCALE = 1.0 / np.sqrt(HEAD_DIM).astype(np.float32)

        def rms_norm(x, g):
            return x * jax.lax.rsqrt(jnp.mean(x * x, axis=-1, keepdims=True) + EPS) * g

        def attention(q, k, v, kv_mask=None):
            s = jnp.einsum('bqhd,bkhd->bhqk', q, k) * SCALE
            if kv_mask is not None:
                s = jnp.where(kv_mask[:, None, None, :], s, jnp.float32(-1000000000.0))
            p = jax.nn.softmax(s, axis=-1)
            return jnp.einsum('bhqk,bkhd->bqhd', p, v)
        b = x.shape[0]
        ctx_img = context[:, :IMG_TOKENS]
        ctx_txt = context[:, IMG_TOKENS:]
        q = rms_norm(x @ w_q.T + b_q, g_q).reshape(b, -1, HEADS, HEAD_DIM)
        k = rms_norm(ctx_txt @ w_k.T + b_k, g_k).reshape(b, -1, HEADS, HEAD_DIM)
        v = (ctx_txt @ w_v.T + b_v).reshape(b, -1, HEADS, HEAD_DIM)
        k_img = rms_norm(ctx_img @ w_k_img.T + b_k_img, g_k_img).reshape(b, -1, HEADS, HEAD_DIM)
        v_img = (ctx_img @ w_v_img.T + b_v_img).reshape(b, -1, HEADS, HEAD_DIM)
        txt_len = ctx_txt.shape[1]
        kv_mask = jnp.arange(txt_len)[None, :] < context_lens[:, None]
        img_x = attention(q, k_img, v_img)
        txt_x = attention(q, k, v, kv_mask)
        out = (txt_x + img_x).reshape(b, -1, DIM)
        return out @ w_o.T + b_o

    def _L0_ffn_ref(hidden_states, router_weight, router_bias, gate_up_proj, gate_up_proj_bias, down_proj, down_proj_bias):
        import jax, jax.numpy as jnp
        import numpy as np
        ALPHA = 1.702
        LIMIT = 7.0
        TOP_K = 2
        E, H, I = (8, 512, 512)
        B, S = (2, 512)
        bsz, seq_len, hidden = hidden_states.shape
        h = hidden_states.reshape(-1, hidden)
        T = h.shape[0]
        logits = h @ router_weight.T + router_bias
        top_vals, top_idx = jax.lax.top_k(logits, TOP_K)
        top_w = jax.nn.softmax(top_vals, axis=-1)
        scores = jnp.zeros_like(logits).at[jnp.arange(T)[:, None], top_idx].set(top_w)
        gate_up = jnp.einsum('th,ehj->etj', h, gate_up_proj) + gate_up_proj_bias[:, None, :]
        gate = gate_up[..., ::2]
        up = gate_up[..., 1::2]
        gate = jnp.minimum(gate, LIMIT)
        up = jnp.clip(up, -LIMIT, LIMIT)
        glu = gate * jax.nn.sigmoid(gate * ALPHA)
        act = (up + 1.0) * glu
        expert_out = jnp.einsum('eti,eih->eth', act, down_proj) + down_proj_bias[:, None, :]
        out = jnp.einsum('te,eth->th', scores, expert_out)
        return out.reshape(bsz, seq_len, hidden)
    x = x + _L0_xattn_ref(_layernorm(x, axis=-1), ctx_2048, _lenS2, L0_xattn_w_q, L0_xattn_b_q, L0_xattn_w_k, L0_xattn_b_k, L0_xattn_w_v, L0_xattn_b_v, L0_xattn_w_k_img, L0_xattn_b_k_img, L0_xattn_w_v_img, L0_xattn_b_v_img, L0_xattn_w_o, L0_xattn_b_o, L0_xattn_g_q, L0_xattn_g_k, L0_xattn_g_k_img)
    x = x + _L0_ffn_ref(_layernorm(x, axis=-1), L0_ffn_router_weight, L0_ffn_router_bias, L0_ffn_gate_up_proj, L0_ffn_gate_up_proj_bias, L0_ffn_down_proj, L0_ffn_down_proj_bias)
    return x

_drawn_inputs = setup_inputs


def setup_inputs(seed=0):
    import zlib

    import numpy as np

    out = dict(_drawn_inputs(seed))
    spreads = {'L0_xattn_b_q': (0.0, 0.749),
     'L0_xattn_b_k': (0.0, 0.1),
     'L0_xattn_b_v': (0.0, 0.1),
     'L0_xattn_b_k_img': (0.0, 0.8),
     'L0_xattn_b_v_img': (0.0, 0.1),
     'L0_xattn_b_o': (0.0, 0.1),
     'L0_xattn_g_q': (1.0, 0.6),
     'L0_xattn_g_k': (1.0, 0.2),
     'L0_xattn_g_k_img': (1.0, 0.6)}
    factors = {'L0_ffn_router_bias': 3.815,
     'L0_ffn_gate_up_proj_bias': 8.0,
     'L0_ffn_down_proj_bias': 4.027}
    for name, (base, spread) in spreads.items():
        noise = np.random.default_rng([zlib.crc32(name.encode()), seed]).standard_normal(out[name].shape)
        drawn = base * np.exp(spread * noise) if base else spread * noise
        out[name] = jnp.asarray(drawn.astype(out[name].dtype))
    for name, factor in factors.items():
        out[name] = (out[name] * factor).astype(out[name].dtype)
    return out
```

```python
from contextlib import ExitStack

import numpy as np

import concourse.bass as bass
from concourse import mybir

F32 = mybir.dt.float32
F32R = mybir.dt.float32r
BF16 = mybir.dt.bfloat16
U32 = mybir.dt.uint32
I32 = mybir.dt.int32
ALU = mybir.AluOpType
ACT = mybir.ActivationFunctionType
AX = mybir.AxisListType.X

B = 8
S = 256
D = 512
NH = 16
HD = 32
C = 4
NE = 8
T = 2048
LN_EPS = 1e-5
RMS_EPS = 1e-6
SCALE = 1.0 / float(np.sqrt(np.float32(HD)))
ALPHA = 1.702
LIMIT = 7.0
NT = 23
ER = 2048
RW = 520
SKIP = 4096
TR = NE * ER // 128
GW = 2048
DW = 2056


def program(nc, x, ctxT, wqkvo, bias, bd3, rwT, wga, wgb, wd, cst, cm, out):
    qs = [nc.dram_tensor(f"qs{b}", (2, HD, NH * S), F32, kind="Internal").ap() for b in range(B)]
    ks = [nc.dram_tensor(f"ks{b}", (2, HD, NH * S), F32, kind="Internal").ap() for b in range(B)]
    vs = [nc.dram_tensor(f"vs{b}", (128, 2 * D), F32, kind="Internal").ap() for b in range(B)]
    hb = nc.dram_tensor("hb", (T, RW), F32, kind="Internal").ap()
    slot = nc.dram_tensor("slot", ((TR + 1) * 128, 1), F32, kind="Internal").ap()

    with ExitStack() as top:
        queues = {n: [] for n in ("tensor", "vector", "scalar", "gpsimd", "sync")}
        done = {n: top.enter_context(nc.semaphore(f"done_{n}")) for n in ("tensor", "vector", "scalar", "gpsimd")}
        count = {n: 0 for n in done}
        dsem = {}
        dcount = {}

        def op(eng, fn, *waits):
            count[eng] += 1
            queues[eng].append((fn, [w for w in waits if w is not None], done[eng], 1))
            return (done[eng], count[eng])

        def pe(fn, *waits):
            return op("tensor", fn, *waits)

        def dve(fn, *waits):
            return op("vector", fn, *waits)

        def act(fn, *waits):
            return op("scalar", fn, *waits)

        def pool(fn, *waits):
            return op("gpsimd", fn, *waits)

        def dma(eng, key, fn, *waits):
            if key not in dsem:
                dsem[key] = top.enter_context(nc.semaphore(f"d_{key}"))
                dcount[key] = 0
            dcount[key] += 16
            queues[eng].append((fn, [w for w in waits if w is not None], dsem[key], 16))
            return (dsem[key], dcount[key])

        def load(key, dst, src, *waits, eng="sync"):
            return dma(eng, key, lambda e: e.dma_start(dst, src), *waits)

        def sb(ctx, name, shape, dt=F32):
            return ctx.enter_context(nc.sbuf_tensor(name, shape, dt))

        bank = [top.enter_context(nc.psum_tensor(f"bank{i}", [128, 512], F32)) for i in range(8)]
        free = [[] for _ in range(8)]

        ident = sb(top, "ident", [128, 128])
        cstt = sb(top, "cstt", [128, 256])
        tri = sb(top, "tri", [128, 128], BF16)
        ones = sb(top, "ones", [128, 128], BF16)
        onef = sb(top, "onef", [128, 32])
        cmt = sb(top, "cmt", [128, cm.shape[1]])
        half = sb(top, "half", [128, 2])
        run = sb(top, "run", [128, NE])
        rw = sb(top, "rw", [128, C * NE])
        t_id = load("cst", ident[:], cst[0])
        t_cm = load("cm", cmt[:], cm)
        t_tr = load("tri", cstt[:, 0:128], cst[1])
        t_rw = load("rw", rw[:], rwT)
        t_tri = dve(lambda e: e.tensor_copy(tri[:], cstt[:, 0:128]), t_tr)
        t_ones = dve(lambda e: e.memset(ones[:], 1.0))
        t_onef = dve(lambda e: e.memset(onef[:], 1.0))
        t_half = dve(lambda e: e.memset(half[:], -0.5))
        IOTA = cmt[:, 0:32].rearrange("p (t j e) -> p t j e", t=2, j=2)
        IO8 = cmt[:, 0:8]
        EBASE = cmt[:, 32:40]
        RB = cmt[:, 40:56]
        PIDX = cmt[:, 56:57]
        MH = cmt[0:24, 57:58]
        ML = cmt[0:24, 58:59]
        TI8 = cmt[:, 136:136 + 8 * NT].rearrange("p (i e) -> p i e", e=8)
        IT8 = cmt[:, 320:320 + 8 * NT].rearrange("p (i e) -> p i e", e=8)
        TOK = cmt[:, 504:520]
        SPT = cmt[:, 60:61]
        SPR = cmt[:, 61:62]
        skips = sb(top, "skips", [128, TR + 1])
        t_skip = pool(lambda e: e.memset(skips[:], float(SKIP)))
        t_slot = load("slot", slot.rearrange("(p n) o -> p (n o)", p=128), skips[:], t_skip)
        t_run = dve(lambda e: e.tensor_copy(run[:], EBASE), t_cm)

        def mm3(o, lh, ll, rh, rl):
            def emit(e):
                n = len(lh)
                last = None
                for c in range(n):
                    for j, (a, b) in enumerate(((lh[c], rh[c]), (lh[c], rl[c]), (ll[c], rh[c]))):
                        last = nc.tensor.matmul(o, a, b, start=(c == 0 and j == 0), stop=(c == n - 1 and j == 2))
                return last
            return emit

        def transposes(o, src, n, np_=128, w=128):
            def emit(e):
                for k in range(n):
                    last = nc.tensor.transpose(o[:, k * np_:(k + 1) * np_], src[:, k * w:(k + 1) * w],
                                               ident[0:np_, 0:np_])
                return last
            return emit

        def split_psum(hi, lo, src, ready, *waits):
            th = act(lambda e: e.activation(hi, src, ACT.Copy), ready, *waits)
            tl = dve(lambda e: e.tensor_tensor(lo, src, hi.bitcast(F32), ALU.subtract), th)
            return th, tl

        v_out = [None] * B
        q_out = [None] * B
        k_out = [None] * B
        wo_ctx = ExitStack()
        whi3 = sb(wo_ctx, "wohi", [128, C * D], F32R)
        wlo3 = sb(wo_ctx, "wolo", [128, C * D], F32R)
        bo = sb(wo_ctx, "bo", [128, D])
        bdh = sb(wo_ctx, "bdh", [24, D], F32R)
        bds = sb(wo_ctx, "bds", [24, D], F32R)
        with ExitStack() as ctx:
            WH = [sb(ctx, f"wh{i}", [128, C * D], F32R) for i in range(3)] + [whi3]
            WL = [sb(ctx, f"wl{i}", [128, C * D], F32R) for i in range(3)] + [wlo3]
            wraw = [sb(ctx, f"wraw{i}", [128, C * D]) for i in range(2)]
            bi = [sb(ctx, f"bi{i}", [128, D]) for i in range(5)]
            bdr = sb(ctx, "bdr", [24, D])
            bdl = sb(ctx, "bdl", [24, D])
            xt = [sb(ctx, f"xt{i}", [128, 2, D]) for i in range(2)]
            st6 = sb(ctx, "st6", [128, 2, 6])
            mv = sb(ctx, "mv", [128, 2, 2])
            ve = sb(ctx, "ve", [128, 2])
            rs = sb(ctx, "rs", [128, 2])
            hn = [sb(ctx, f"hn{i}", [128, D]) for i in range(2)]
            hth = [sb(ctx, f"hth{i}", [128, C, S], F32R) for i in range(2)]
            htl = [sb(ctx, f"htl{i}", [128, C, S], F32R) for i in range(2)]
            cr = [sb(ctx, f"cr{i}", [128, C * S]) for i in range(2)]
            cth = [sb(ctx, f"cth{i}", [128, C * S], F32R) for i in range(2)]
            ctl = [sb(ctx, f"ctl{i}", [128, C * S], F32R) for i in range(2)]
            pf = [sb(ctx, f"pf{i}", [128, D]) for i in range(4)]
            sqj = sb(ctx, "sqj", [128, D])
            ss = [sb(ctx, f"ss{i}", [128, 1]) for i in range(4)]
            sr = [sb(ctx, f"sr{i}", [128, 1]) for i in range(4)]
            qth = [sb(ctx, f"qth{i}", [128, C, S], F32R) for i in range(2)]
            qtl = [sb(ctx, f"qtl{i}", [128, C, S], F32R) for i in range(2)]
            vt = [sb(ctx, f"vt{i}", [128, 2 * D]) for i in range(2)]

            x_in = {}
            x_free = [None, None]
            c_in = {}
            c_free = [[], []]
            ht_free = [None, None]
            ct_free = [None, None]
            hn_free = [None, None]

            def load_batch(b):
                p = b % 2
                x_in[b] = load(f"x{p}", xt[p][:], x[b * S:(b + 1) * S, :].rearrange("(t p) d -> p t d", p=128), x_free[p])
                c_in[b] = load(f"c{p}", cr[p][:], ctxT[b], *c_free[p])

            load_batch(0)
            b_in = None
            w_t = {}

            def load_w(i, p, *waits):
                return load(f"w{p}", wraw[p][:], wqkvo[i], *waits)

            def split_w(i, p, ready):
                th = act(lambda e: e.activation(WH[i][:], wraw[p][:], ACT.Copy), ready)
                tl = dve(lambda e: e.tensor_tensor(WL[i][:], wraw[p][:], WH[i][:].bitcast(F32), ALU.subtract), th)
                w_t[i] = (th, tl)
                return tl

            w0 = load_w(0, 0)
            w1 = load_w(1, 1)
            for i, dst in enumerate(bi):
                b_in = load("bi", dst[:], bias[i])
            b_in = load("bi", bo[:], bias[5])
            t_bd = load("bd", bdr[:], bd3)
            load_batch(1)

            ht_t = {}
            ct_t = {}
            ring = {"m": 0, "t": 0}

            def mbank():
                ring["m"] += 1
                return (ring["m"] - 1) % 4

            def tbank():
                ring["t"] += 1
                return 4 + (ring["t"] - 1) % 4

            def layer_norm(b):
                p = b % 2
                for t in range(2):
                    s_ = dve(lambda e, t=t: e.bn_stats(st6[:, t, :], xt[p][:, t, :]), x_in[b], ln_free[0])
                for t in range(2):
                    a_ = dve(lambda e, t=t: e.bn_aggr(mv[:, t, :], st6[:, t, :]), s_)
                v_ = dve(lambda e: e.tensor_scalar(ve[:], mv[:, :, 1], LN_EPS, None, ALU.add), a_)
                r_ = pool(lambda e: e.tensor_tensor(rs[:], ve[:], half[:], ALU.pow), v_, t_half)
                for t in range(2):
                    n_ = dve(lambda e, t=t: e.tensor_scalar(hn[t][:], xt[p][:, t, :], mv[:, t, 0:1], rs[:, t:t + 1],
                                                            ALU.subtract, ALU.mult), r_, hn_free[t])
                    ln_t[(b, t)] = n_
                ln_free[0] = n_
                x_free[p] = n_

            ln_free = [None]
            ln_t = {}

            def ln_transposes(b):
                p = b % 2
                for t in range(2):
                    k = tbank()
                    g = pe(transposes(bank[k], hn[t], 4), ln_t[(b, t)], t_id, *free[k])
                    hn_free[t] = g
                    src = bank[k][:].rearrange("p (c n) -> p c n", c=4)
                    th, tl = split_psum(hth[p][:, :, t * 128:(t + 1) * 128], htl[p][:, :, t * 128:(t + 1) * 128],
                                        src, g, ht_free[p])
                    free[k] = [th, tl]
                ht_t[b] = (th, tl)

            def ctx_split(b):
                p = b % 2
                th = act(lambda e: e.activation(cth[p][:], cr[p][:], ACT.Copy), c_in[b], ct_free[p])
                tl = dve(lambda e: e.tensor_tensor(ctl[p][:], cr[p][:], cth[p][:].bitcast(F32), ALU.subtract), th)
                ct_t[b] = (th, tl)
                c_free[p] = [th, tl]

            layer_norm(0)
            ctx_split(0)
            r0 = split_w(0, 0, w0)
            w2 = load_w(2, 0, r0)
            r1 = split_w(1, 1, w1)
            w3 = load_w(3, 1, r1)
            ln_transposes(0)
            r2 = split_w(2, 0, w2)
            later = [lambda: split_w(3, 1, w3)]

            def bd_split():
                th = act(lambda e: e.activation(bdh[:], bdr[:], ACT.Copy), t_bd)
                tl = dve(lambda e: e.tensor_tensor(bdl[:], bdr[:], bdh[:].bitcast(F32), ALU.subtract), th)
                tm = dve(lambda e: e.tensor_scalar(bdl[:], bdl[:], ML, None, ALU.mult), tl, t_cm)
                return dve(lambda e: e.scalar_tensor_tensor(out=bds[:], in0=bdh[:].bitcast(F32), scalar=MH, in1=bdl[:],
                                                            op0=ALU.mult, op1=ALU.add), tm)

            pf_free = [None] * 4
            qt_free = [None, None]
            vt_free = [None, None]
            units = 0

            def project(b, kind, t):
                nonlocal units
                p = b % 2
                k = mbank()
                if kind == 0:
                    lh = [hth[p][:, c, t * 128:(t + 1) * 128] for c in range(C)]
                    ll = [htl[p][:, c, t * 128:(t + 1) * 128] for c in range(C)]
                    ready = ht_t[b]
                else:
                    lh = [cth[p][:, c * S + t * 128:c * S + (t + 1) * 128] for c in range(C)]
                    ll = [ctl[p][:, c * S + t * 128:c * S + (t + 1) * 128] for c in range(C)]
                    ready = ct_t[b]
                rh = [WH[kind][:, c * D:(c + 1) * D] for c in range(C)]
                rl = [WL[kind][:, c * D:(c + 1) * D] for c in range(C)]
                g = pe(mm3(bank[k][:], lh, ll, rh, rl), *ready, *w_t[kind], *free[k])
                if kind == 2:
                    a = dve(lambda e: e.tensor_tensor(vt[p][:, t * D:(t + 1) * D], bank[k][:], bi[2][:], ALU.add),
                            g, b_in, vt_free[p])
                    free[k] = [a]
                    return g, a
                u = units % 4
                units += 1
                a = dve(lambda e: e.tensor_tensor(pf[u][:], bank[k][:], bi[kind][:], ALU.add), g, b_in, pf_free[u])
                free[k] = [a]
                s_ = act(lambda e: e.activation(sqj[:], pf[u][:], ACT.Square, accum_out=ss[u][:]), a)
                m_ = dve(lambda e: e.tensor_scalar(ss[u][:], ss[u][:], 1.0 / D, RMS_EPS, ALU.mult, ALU.add), s_)
                r_ = pool(lambda e: e.tensor_tensor(sr[u][:], ss[u][:], half[:, 0:1], ALU.pow), m_, t_half)
                return g, (u, r_)

            def normalise(kind, u, r_):
                return dve(lambda e: e.scalar_tensor_tensor(out=pf[u][:], in0=pf[u][:], scalar=sr[u][:, 0:1],
                                                            in1=bi[3 + kind][:], op0=ALU.mult, op1=ALU.mult), r_)

            def to_heads(b, kind, t, u, n_):
                k = tbank()
                g = pe(transposes(bank[k], pf[u], 4), n_, *free[k])
                pf_free[u] = g
                src = bank[k][:].rearrange("p (c n) -> p c n", c=4)
                th, tl = split_psum(qth[kind][:, :, t * 128:(t + 1) * 128], qtl[kind][:, :, t * 128:(t + 1) * 128],
                                    src, g, qt_free[kind])
                free[k] = [th, tl]
                return th, tl

            def store_heads(b, kind, th, tl):
                dst = (qs if kind == 0 else ks)[b]
                for n, (tile, tok) in enumerate(((qth[kind], th), (qtl[kind], tl))):
                    for h4 in range(4):
                        o = dst[n].rearrange("d (h m) -> d h m", h=4)[:, h4, :]
                        i = tile[32 * h4:32 * h4 + 32, :, :].bitcast(F32).rearrange("p c n -> p (c n)")
                        z = load(f"s{kind}", o, i, tok)
                qt_free[kind] = z
                (q_out if kind == 0 else k_out)[b] = z

            for b in range(B):
                p = b % 2
                if b + 1 < B:
                    layer_norm(b + 1)
                _, q0 = project(b, 0, 0)
                _, k0 = project(b, 1, 0)
                nq0 = normalise(0, *q0)
                _, _ = project(b, 2, 0)
                nk0 = normalise(1, *k0)
                to_heads(b, 0, 0, q0[0], nq0)
                gq, q1 = project(b, 0, 1)
                ht_free[p] = gq
                to_heads(b, 1, 0, k0[0], nk0)
                _, k1 = project(b, 1, 1)
                nq1 = normalise(0, *q1)
                if b + 1 < B:
                    ln_transposes(b + 1)
                gv, vv = project(b, 2, 1)
                ct_free[p] = gv
                vt_free[p] = v_out[b] = load(f"v{p}", vs[b], vt[p][:], vv)
                nk1 = normalise(1, *k1)
                store_heads(b, 0, *to_heads(b, 0, 1, q1[0], nq1))
                if b + 1 < B:
                    ctx_split(b + 1)
                store_heads(b, 1, *to_heads(b, 1, 1, k1[0], nk1))
                if b + 2 < B:
                    load_batch(b + 2)
                if b == 0:
                    later[0]()
                    t_bds = bd_split()
            over_a = [(done[n], count[n]) for n in ("tensor", "vector", "scalar", "gpsimd")] + \
                     [(dsem[k], dcount[k]) for k in ("s0", "s1", "v0", "v1")]

        with ExitStack() as ctx:
            qst = [sb(ctx, f"qst{i}", [128, NH, S], F32R) for i in range(3)]
            kst = [sb(ctx, f"kst{i}", [128, NH, S], F32R) for i in range(3)]
            vb = [sb(ctx, f"vb{i}", [128, 2 * D]) for i in range(3)]
            mx = [sb(ctx, f"mx{i}", [128, 2, NH]) for i in range(2)]
            nm = [sb(ctx, f"nm{i}", [NH, 2, 128]) for i in range(2)]
            pt = [sb(ctx, f"pt{i}", [128, 512]) for i in range(6)]
            rec = [sb(ctx, f"rec{i}", [128, S]) for i in range(1)]
            of = [sb(ctx, f"of{i}", [128, S]) for i in range(2)]
            oh_ = [sb(ctx, f"oh{i}", [128, C, S], F32R) for i in range(2)]
            ol_ = [sb(ctx, f"ol{i}", [128, C, S], F32R) for i in range(1)]
            xb = [sb(ctx, f"xb{i}", [128, D]) for i in range(2)]
            hr = [sb(ctx, f"hr{i}", [128, RW]) for i in range(2)]
            h2t = sb(ctx, "h2t", [128, 512])
            st6B = sb(ctx, "st6b", [128, 6])
            mvB = sb(ctx, "mvb", [128, 2])
            veB = sb(ctx, "veb", [128, 1])
            rsB = sb(ctx, "rsb", [128, 1])
            lg = sb(ctx, "lg", [128, 2, NE])
            m8 = sb(ctx, "m8", [128, 2, 8])
            ix = sb(ctx, "ix", [128, 2, 8], U32)
            ixf = sb(ctx, "ixf", [128, 2, 8])
            oht = sb(ctx, "oht", [128, 2, 2, NE])
            dd = sb(ctx, "dd", [128, 2])
            ee = sb(ctx, "ee", [128, 2])
            se = sb(ctx, "se", [128, 2])
            wa = sb(ctx, "wa", [128, 2])
            wb = sb(ctx, "wb", [128, 2])
            tmp8 = sb(ctx, "tmp8", [128, 2, NE])
            M = sb(ctx, "M", [128, 2, NE], BF16)
            pos = sb(ctx, "pos", [128, 2, NE])
            pr = sb(ctx, "pr", [128, 2, 2, NE])
            sl = sb(ctx, "sl", [128, 4])
            si = [sb(ctx, f"si{i}", [128, 4], U32) for i in range(2)]
            sc3 = sb(ctx, "sc3", [128, 2, 3, NE])
            s3t = sb(ctx, "s3t", [24, 256], F32R)
            ob = [sb(ctx, f"ob{i}", [128, D]) for i in range(2)]

            st_in = {}
            st_free = [over_a, over_a, over_a]
            v_in = {}
            one_t = []
            for i in range(3):
                one_t.append(dve(lambda e, i=i: e.memset(kst[i][96:97, :, :].bitcast(F32), 1.0), *(over_a if i == 0 else ())))

            def load_stacks(b):
                i = b % 3
                w = list(st_free[i])
                for n, (dst, src, tok, part) in enumerate(((qst, qs, q_out, (0, 0, 1)), (kst, ks, k_out, (0, 1, 0)))):
                    for quad, plane in enumerate(part):
                        st_in[b] = load(f"st{i}", dst[i][32 * quad:32 * quad + 32, :, :].bitcast(F32)
                                        .rearrange("p h n -> p (h n)"), src[b][plane], tok[b], *w)
                v_in[b] = load(f"vb{i}", vb[i][:], vs[b], v_out[b], *w)

            mx_t = {}
            nm_t = {}
            m_in = {}
            mx_free = [over_a, over_a]

            def head(b, cb, h4):
                return h4 * 4 + cb

            def score_max(b, n):
                cb, h4 = divmod(n, 4)
                s_ = head(b, cb, h4)
                i = b % 3
                k = n % 2
                def emit(e):
                    for t in range(2):
                        last = nc.tensor.matmul(bank[k][:, t * 256:(t + 1) * 256],
                                                qst[i][0:96, s_, t * 128:(t + 1) * 128], kst[i][0:96, s_, :],
                                                start=True, stop=True)
                    return last
                g = pe(emit, st_in[b], *free[k])
                d_ = dve(lambda e: e.tensor_reduce(mx[b % 2][:, :, s_], bank[k][:].rearrange("p (t n) -> p t n", t=2),
                                                   AX, ALU.max), g, *mx_free[b % 2])
                free[k] = [d_]
                mx_t[b] = d_

            def send_max(b):
                k = ubank()
                def emit(e):
                    for t in range(2):
                        last = nc.tensor.transpose(bank[k][0:NH, t * 128:(t + 1) * 128], mx[b % 2][:, t, :], ident[:])
                    return last
                g = pe(emit, mx_t[b], *free[k])
                mx_free[b % 2] = [g]
                a_ = act(lambda e: e.activation(nm[b % 2][:].rearrange("h t n -> h (t n)"), bank[k][0:NH, 0:256],
                                                ACT.Copy, scale=-1.0), g, m_in.get(b - 2))
                free[k] = [a_]
                m_in[b] = load(f"m{b % 2}", qst[b % 3][96:97, :, :].bitcast(F32),
                               nm[b % 2][:].rearrange("h t n -> h (t n)"), a_)

            ub = [0]

            def ubank():
                ub[0] += 1
                return 6 + (ub[0] - 1) % 2

            pt_free = [None] * 6
            pt_t = {}
            pn = [0]

            def probs(b, n):
                cb, h4 = divmod(n, 4)
                s_ = head(b, cb, h4)
                i = b % 3
                k = 2 + n % 2
                u = pn[0] % 6
                pn[0] += 1
                def emit(e):
                    for t in range(2):
                        last = nc.tensor.matmul(bank[k][:, t * 256:(t + 1) * 256],
                                                kst[i][0:97, s_, t * 128:(t + 1) * 128], qst[i][0:97, s_, :],
                                                start=True, stop=True)
                    return last
                g = pe(emit, st_in[b], m_in[b], one_t[2], *free[k])
                a_ = act(lambda e: e.activation(pt[u][:], bank[k][:], ACT.Exp, scale=SCALE), g, pt_free[u])
                free[k] = [a_]
                pt_t[(b, n)] = (u, a_)
                return g

            o_t = {}
            of_free = [None, None]
            o_free = [None, None]
            gn = [0]

            def values(b, g4):
                k = 4 + gn[0] % 2
                f = gn[0] % 2
                gn[0] += 1
                us = [pt_t[(b, 4 * g4 + j)] for j in range(4)]
                def emit(e):
                    for half_ in range(2):
                        for t in range(2):
                            for j in range(4):
                                lhs = onef[:] if half_ else vb[b % 3][:, t * D + g4 * 128 + 32 * j:t * D + g4 * 128 + 32 * j + 32]
                                last = nc.tensor.matmul(bank[k][32 * j:32 * j + 32, half_ * 256:half_ * 256 + 256], lhs,
                                                        pt[us[j][0]][:, t * 256:(t + 1) * 256],
                                                        start=(t == 0), stop=(t == 1))
                    return last
                g = pe(emit, *[u[1] for u in us], v_in[b], t_onef, *free[k])
                for u in us:
                    pt_free[u[0]] = g
                r_ = dve(lambda e: e.reciprocal(rec[0][:], bank[k][:, 256:512]), g)
                m_ = dve(lambda e: e.tensor_tensor(of[f][:], bank[k][:, 0:256], rec[0][:], ALU.mult), r_, of_free[f])
                free[k] = [m_]
                h_ = act(lambda e: e.activation(oh_[b % 2][:, g4, :], of[f][:], ACT.Copy), m_, o_free[b % 2])
                l_ = pool(lambda e: e.tensor_tensor(ol_[0][:, g4, :], of[f][:], oh_[b % 2][:, g4, :].bitcast(F32),
                                                    ALU.subtract), h_, o_free[(b + 1) % 2])
                of_free[f] = l_
                o_t[b] = (h_, l_)
                return g

            xb_free = [None, None]
            xb_in = {}
            hr_free = [None, None]
            x2_t = {}
            h2_t = {}
            ob_free = [None, None]
            base_out = []
            lg_t = {}

            def load_x(b):
                for t in range(2):
                    xb_in[(b, t)] = load(f"xb{t}", xb[t][:], x[b * S + t * 128:b * S + (t + 1) * 128, :], xb_free[t],
                                         *(over_a if b == 0 else ()))

            def out_project(b, t):
                k = ubank()
                lh = [oh_[b % 2][:, c, t * 128:(t + 1) * 128] for c in range(C)]
                ll = [ol_[0][:, c, t * 128:(t + 1) * 128] for c in range(C)]
                rh = [whi3[:, c * D:(c + 1) * D] for c in range(C)]
                rl = [wlo3[:, c * D:(c + 1) * D] for c in range(C)]
                g = pe(mm3(bank[k][:], lh, ll, rh, rl), *o_t[b], *w_t[3], *free[k])
                if t == 1:
                    o_free[b % 2] = g
                p_ = pool(lambda e: e.tensor_tensor(xb[t][:], xb[t][:], bo[:], ALU.add), xb_in[(b, t)], b_in)
                a_ = dve(lambda e: e.tensor_tensor(xb[t][:], bank[k][:], xb[t][:], ALU.add), g, p_)
                free[k] = [a_]
                s_ = dve(lambda e: e.bn_stats(st6B[:], xb[t][:]), a_)
                s_ = dve(lambda e: e.bn_aggr(mvB[:], st6B[:]), s_)
                v_ = dve(lambda e: e.tensor_scalar(veB[:], mvB[:, 1:2], LN_EPS, None, ALU.add), s_)
                r_ = pool(lambda e: e.tensor_tensor(rsB[:], veB[:], half[:, 0:1], ALU.pow), v_)
                h_ = dve(lambda e: e.tensor_scalar(hr[t][:, 0:512], xb[t][:], mvB[:, 0:1], rsB[:, 0:1],
                                                   ALU.subtract, ALU.mult), r_, hr_free[t])
                x2_t[(b, t)] = a_
                h2_t[(b, t)] = h_

            h2t_free = [None]

            def router(b, t):
                k = ubank()
                g = pe(transposes(bank[k], hr[t], 4), h2_t[(b, t)], *free[k])
                a_ = act(lambda e: e.activation(h2t[:], bank[k][:], ACT.Copy), g, h2t_free[0])
                free[k] = [a_]
                k2 = lgb[0]
                def emit(e):
                    for c in range(C):
                        last = nc.tensor.matmul(bank[k2][:, t * 8:t * 8 + 8], h2t[:, c * 128:(c + 1) * 128],
                                                rw[:, c * NE:(c + 1) * NE], start=(c == 0), stop=(c == C - 1))
                    return last
                g = pe(emit, a_, t_rw, *free[k2])
                h2t_free[0] = g
                free[k2] = [g]
                lg_t[(b, t)] = g

            lgb = [0]
            rk = [None]
            si_free = [None, None]
            pass

            def choose(b):
                k2 = lgb[0]
                c_ = dve(lambda e: e.tensor_tensor(lg[:].rearrange("p t e -> p (t e)"), bank[k2][:, 0:16], RB, ALU.add),
                         lg_t[(b, 0)], lg_t[(b, 1)])
                free[k2] = [c_]
                for t in range(2):
                    m_ = dve(lambda e, t=t: e.max(m8[:, t, :], lg[:, t, :]), c_)
                d_ = dve(lambda e: e.tensor_tensor(dd[:], m8[:, :, 1], m8[:, :, 0], ALU.subtract), m_)
                e_ = act(lambda e: e.activation(ee[:], dd[:], ACT.Exp), d_)
                for t in range(2):
                    i_ = dve(lambda e, t=t: e.max_index(ix[:, t, :], m8[:, t, :], lg[:, t, :]), m_)
                f_ = dve(lambda e: e.tensor_copy(ixf[:], ix[:]), i_)
                o_ = dve(lambda e: e.tensor_tensor(oht[:], IOTA, ixf[:, :, 0:2].unsqueeze(3).to_broadcast([128, 2, 2, NE]),
                                                   ALU.is_equal), f_)
                M_ = dve(lambda e: e.tensor_tensor(M[:], oht[:, :, 0, :], oht[:, :, 1, :], ALU.add), o_, rk[0])
                s_ = dve(lambda e: e.tensor_scalar(se[:], ee[:], 1.0, None, ALU.add), e_)
                w_ = dve(lambda e: e.reciprocal(wa[:], se[:]), s_)
                w2_ = dve(lambda e: e.tensor_tensor(wb[:], ee[:], wa[:], ALU.mult), w_)
                for t in range(2):
                    a_ = dve(lambda e, t=t: e.tensor_scalar(tmp8[:, t, :], oht[:, t, 0, :], wa[:, t:t + 1], None, ALU.mult), w_)
                for t in range(2):
                    y_ = dve(lambda e, t=t: e.scalar_tensor_tensor(out=hr[t][:, 512:520], in0=oht[:, t, 1, :],
                                                                   scalar=wb[:, t:t + 1], in1=tmp8[:, t, :],
                                                                   op0=ALU.mult, op1=ALU.add), a_, w2_, *([hr_free[t]]))
                for t in range(2):
                    z_ = dve(lambda e, t=t: e.tensor_copy(sc3[:, t, 0, :].bitcast(F32R), hr[t][:, 512:520]), y_, s3_free[0])
                for t in range(2):
                    z1 = dve(lambda e, t=t: e.tensor_copy(sc3[:, t, 1, :], sc3[:, t, 0, :]), z_)
                    z2 = dve(lambda e, t=t: e.tensor_tensor(sc3[:, t, 2, :], hr[t][:, 512:520], sc3[:, t, 0, :], ALU.subtract), z_)
                return M_, y_, z2

            s3_free = [None]
            s3t_free = [None]

            def rank(b, M_, y_, z2):
                k = ubank()
                def emit(e):
                    r = bank[k]
                    nc.tensor.matmul(r[:, 0:8], tri[:], M[:, 0, :], start=True, stop=True)
                    nc.tensor.matmul(r[:, 8:16], tri[:], M[:, 1, :], start=True, stop=False)
                    nc.tensor.matmul(r[:, 8:16], ones[:], M[:, 0, :], start=False, stop=True)
                    nc.tensor.matmul(r[:, 16:24], ones[:], M[:, 0, :], start=True, stop=False)
                    return nc.tensor.matmul(r[:, 16:24], ones[:], M[:, 1, :], start=False, stop=True)
                g = pe(emit, M_, t_tri, t_ones, *free[k])
                rk[0] = g
                p_ = dve(lambda e: e.tensor_tensor(pos[:], bank[k][:, 0:16].rearrange("p (t e) -> p t e", t=2),
                                                   run[:].unsqueeze(1).to_broadcast([128, 2, NE]), ALU.add), g, t_run, run_t[0])
                n_ = dve(lambda e: e.tensor_tensor(run[:], bank[k][:, 16:24], run[:], ALU.add), p_)
                run_t[0] = n_
                free[k] = [n_]
                q_ = dve(lambda e: e.tensor_tensor(pr[:], oht[:], pos[:].unsqueeze(2).to_broadcast([128, 2, 2, NE]), ALU.mult), p_)
                r_ = dve(lambda e: e.tensor_reduce(sl[:], pr[:].rearrange("p t j e -> p (t j) e"), AX, ALU.add), q_)
                i_ = dve(lambda e: e.tensor_copy(si[b % 2][:], sl[:]), r_, si_free[b % 2])
                for t in range(2):
                    for j in range(2):
                        n = 2 * t + j
                        z = dma("gpsimd", f"sc{b % 2}", lambda e, n=n, t=t: e.indirect_dma_start(
                            slot, bass.IndirectOffsetOnAxis(ap=si[b % 2][:, n:n + 1], axis=0),
                            TOK[:, 2 * b + t:2 * b + t + 1], None), i_, t_slot)
                    hr_free[t] = load(f"hr{t}", hb[b * S + t * 128:b * S + (t + 1) * 128, :], hr[t][:], y_)
                si_free[b % 2] = z

            run_t = [None]

            def add_bias(b, z2):
                k = ubank()
                def emit(e):
                    for t in range(2):
                        last = nc.tensor.transpose(bank[k][0:24, t * 128:(t + 1) * 128],
                                                   sc3[:, t, :, :].rearrange("p a e -> p (a e)"), ident[:])
                    return last
                g = pe(emit, z2, *free[k])
                s3_free[0] = g
                a_ = act(lambda e: e.activation(s3t[:], bank[k][0:24, 0:256], ACT.Copy), g, s3t_free[0])
                free[k] = [a_]
                for t in range(2):
                    k = ubank()
                    g = pe(lambda e, t=t, k=k: nc.tensor.matmul(bank[k][:], s3t[:, t * 128:(t + 1) * 128], bds[:],
                                                                start=True, stop=True), a_, t_bds, *free[k])
                    d_ = dve(lambda e, t=t, k=k: e.tensor_tensor(ob[t][:], bank[k][:], xb[t][:], ALU.add), g, ob_free[t])
                    free[k] = [d_]
                    xb_free[t] = d_
                    ob_free[t] = load(f"ob{t}", out[b * S + t * 128:b * S + (t + 1) * 128, :], ob[t][:], d_)
                s3t_free[0] = g
                base_out.append(ob_free[0])
                base_out.append(ob_free[1])

            load_stacks(0)
            load_x(0)
            load_stacks(1)
            hold = {}
            for step in range(-1, B + 1):
                bB, bC, bD = step + 1, step, step - 1
                for n in range(NH):
                    if bB < B:
                        score_max(bB, n)
                    if 0 <= bC < B:
                        gp = probs(bC, n)
                        if n >= 5 and n % 4 == 1:
                            values(bC, n // 4 - 1)
                    if 0 <= bD < B:
                        if n == 2:
                            out_project(bD, 0)
                        if n == 3:
                            out_project(bD, 1)
                if 0 <= bC < B:
                    gv = values(bC, 3)
                    st_free[bC % 3] = [gv]
                if bB < B:
                    send_max(bB)
                if 0 <= bD < B:
                    router(bD, 0)
                    router(bD, 1)
                    M_, y_, z2 = choose(bD)
                    rank(bD, M_, y_, z2)
                    add_bias(bD, z2)
                    if bD + 1 < B:
                        load_x(bD + 1)
                if bC >= 0 and bC + 3 < B:
                    load_stacks(bC + 3)
                if step == -1:
                    load_stacks(2)
            over_b = [(done[n], count[n]) for n in ("tensor", "vector", "scalar", "gpsimd")] + base_out[-2:] + \
                     [(dsem[k], dcount[k]) for k in ("sc0", "sc1", "hr0", "hr1")]
        wo_ctx.close()

        with ExitStack() as ctx:
            raw = [sb(ctx, f"raw{i}", [128, DW]) for i in range(3)]
            wh = [sb(ctx, f"eh{i}", [128, 3, GW], F32R) for i in range(2)]
            wl = [sb(ctx, f"el{i}", [128, 3, GW], F32R) for i in range(2)]
            gb = [sb(ctx, f"gb{i}", [128, 8]) for i in range(2)]
            xs = [sb(ctx, f"xs{i}", [128, 2, RW]) for i in range(2)]
            xh = [sb(ctx, f"xh{i}", [128, C, S], F32R) for i in range(2)]
            xl = [sb(ctx, f"xl{i}", [128, C, S], F32R) for i in range(2)]
            ga = [sb(ctx, f"ga{i}", [128, S]) for i in range(2)]
            up = [sb(ctx, f"up{i}", [128, S]) for i in range(2)]
            sg = [sb(ctx, f"sg{i}", [128, S]) for i in range(2)]
            ah = [sb(ctx, f"ah{i}", [128, C, S], F32R) for i in range(2)]
            al = [sb(ctx, f"al{i}", [128, C, S], F32R) for i in range(2)]
            ys = [sb(ctx, f"ys{i}", [128, D]) for i in range(2)]
            ww = [sb(ctx, f"ww{i}", [128, 2]) for i in range(2)]
            pw = sb(ctx, "pw", [128, 2, NE])
            gk = sb(ctx, "gk", [128, 4])
            gj = sb(ctx, "gj", [128, NE])
            gi = sb(ctx, "gi", [128, 1], U32)
            tab = sb(ctx, "tab", [2 * NT, 128])
            ids = sb(ctx, "ids", [128, 2 * NT])
            ti = sb(ctx, "ti", [128, 2 * NT], U32)
            cn = sb(ctx, "cn", [128, NE])
            ci = sb(ctx, "ci", [128, NE], I32)
            cj = sb(ctx, "cj", [128, NE], I32)
            nt = sb(ctx, "nt", [128, NE])
            en = sb(ctx, "en", [128, NE])
            sn = sb(ctx, "sn", [128, NE])
            b8 = sb(ctx, "b8", [128, NT, NE])
            Ei = sb(ctx, "Ei", [128, NT])
            ohE = sb(ctx, "ohE", [128, NT, NE])
            e0 = sb(ctx, "e0", [128, 1])
            pd = sb(ctx, "pd", [128, NT])
            gx = sb(ctx, "gx", [128, 2 * NT], U32)
            wx = sb(ctx, "wx", [128, NT], U32)
            ba = sb(ctx, "ba", [128, NT])

            def bc(ap, n):
                return ap.unsqueeze(2).to_broadcast([128, NT, n])

            def ch(fn, *w):
                last[0] = dve(fn, last[0], *w)
                return last[0]

            last = [run_t[0]]
            ch(lambda e: e.tensor_tensor(cn[:], run[:], EBASE, ALU.subtract), *over_b)
            ch(lambda e: e.tensor_scalar(ci[:], cn[:], 255.0, None, ALU.add))
            ch(lambda e: e.tensor_scalar(cj[:], ci[:], 8, None, ALU.logical_shift_right))
            ch(lambda e: e.tensor_copy(nt[:], cj[:]))
            ch(lambda e: e.tensor_tensor_scan(en[:], onef[:, 0:NE], nt[:], 0.0, ALU.mult, ALU.add), t_onef)
            ch(lambda e: e.tensor_tensor(sn[:], en[:], nt[:], ALU.subtract))
            ch(lambda e: e.tensor_tensor(b8[:], TI8, en[:].unsqueeze(1).to_broadcast([128, NT, NE]), ALU.is_ge))
            ch(lambda e: e.tensor_reduce(Ei[:], b8[:], AX, ALU.add))
            ch(lambda e: e.tensor_tensor(ohE[:], IT8, bc(Ei[:], NE), ALU.is_equal))
            ch(lambda e: e.tensor_scalar(gj[:], en[:], SPT, None, ALU.is_le))
            ch(lambda e: e.tensor_reduce(gk[:, 0:1], gj[:], AX, ALU.add))
            ch(lambda e: e.tensor_scalar(gj[:], IO8, gk[:, 0:1], None, ALU.is_equal))
            ch(lambda e: e.tensor_tensor(gj[:], gj[:], sn[:], ALU.mult))
            ch(lambda e: e.tensor_reduce(gk[:, 1:2], gj[:], AX, ALU.add))
            ch(lambda e: e.tensor_scalar(gk[:, 2:3], gk[:, 0:1], float(ER // 128), SPR, ALU.mult, ALU.add))
            ch(lambda e: e.scalar_tensor_tensor(out=gk[:, 3:4], in0=gk[:, 1:2], scalar=-2.0, in1=gk[:, 2:3],
                                                op0=ALU.mult, op1=ALU.add))
            ch(lambda e: e.tensor_scalar(gk[:, 2:3], gk[:, 3:4], float(TR), None, ALU.min))
            t_gi = ch(lambda e: e.tensor_copy(gi[:], gk[:, 2:3]))
            t_tab = dma("gpsimd", "tab", lambda e: e.indirect_dma_start(
                tab[:], None, slot.rearrange("(a n) o -> a (n o)", n=128),
                bass.IndirectOffsetOnAxis(ap=gi[0:2 * NT, :], axis=0)), t_gi, *over_b)
            ch(lambda e: e.tensor_scalar(e0[:], Ei[:, 0:1], -float(NE), None, ALU.add))
            ch(lambda e: e.tensor_scalar(pd[:], Ei[:], float(NE), e0[:, 0:1], ALU.is_equal, ALU.mult))
            ch(lambda e: e.tensor_tensor(Ei[:], Ei[:], pd[:], ALU.add))
            ch(lambda e: e.tensor_tensor(ohE[:], IT8, bc(Ei[:], NE), ALU.is_equal))
            ch(lambda e: e.tensor_scalar(ba[:], Ei[:], 128.0, PIDX, ALU.mult, ALU.add))
            t_wx = ch(lambda e: e.tensor_copy(wx[:], ba[:]))
            g_ids = pe(lambda e: nc.tensor.transpose(bank[0][:, 0:2 * NT], tab[:], ident[0:2 * NT, 0:2 * NT]), t_tab, *free[0])
            ch(lambda e: e.tensor_copy(ids[:], bank[0][:, 0:2 * NT]), g_ids)
            free[0] = [last[0]]
            t_ti = ch(lambda e: e.tensor_copy(ti[:], ids[:]))
            ch(lambda e: e.tensor_scalar(ids[:], ids[:], float(T - 1), None, ALU.min))
            t_gx = ch(lambda e: e.tensor_copy(gx[:], ids[:]))

            raw_free = [None] * 3
            wh_free = [None, None]
            gb_free = [None, None]
            xs_free = [[], []]
            xs_in = {}
            w_ok = {}
            rn = [0]

            def gather(key, dst, src, idx, *w):
                return dma("gpsimd", key, lambda e: e.indirect_dma_start(
                    dst, None, src, bass.IndirectOffsetOnAxis(ap=idx, axis=0)), *w)

            def fetch_x(i):
                for r in range(2):
                    z = gather(f"xs{i % 2}", xs[i % 2][:, r, :], hb, gx[:, 2 * i + r:2 * i + r + 1], t_gx, *xs_free[i % 2],
                               *(over_b if i < 2 else ()))
                xs_in[i] = z

            def fetch_w(i, part):
                src = (wga, wgb, wd)[part]
                n = GW if part < 2 else DW
                z = gather(f"raw{part}", raw[part][:, 0:n], src, wx[:, i:i + 1], t_wx, *(raw_free[part] or ()),
                           *(over_b if i == 0 else ()))
                w_in[(i, part)] = z

            w_in = {}

            def split_expert(i, part):
                p = i % 2
                z = w_in[(i, part)]
                th = act(lambda e: e.activation(wh[p][:, part, :], raw[part][:, 0:GW], ACT.Copy), z, wh_free[p])
                tl = dve(lambda e: e.tensor_tensor(wl[p][:, part, :], raw[part][:, 0:GW], wh[p][:, part, :].bitcast(F32),
                                                   ALU.subtract), th)
                toks = [th, tl]
                if part == 2:
                    tb = dve(lambda e: e.tensor_copy(gb[p][:], raw[2][:, GW:DW]), z, gb_free[p])
                    toks.append(tb)
                raw_free[part] = toks
                w_ok[(i, part)] = toks

            x_ok = {}
            xh_free = [None, None]
            ww_free = [None, None]
            ww_t = {}

            def turn_x(i):
                p = i % 2
                for r in range(2):
                    k = 4 + r
                    g = pe(transposes(bank[k], xs[p][:, r, :], 4), xs_in[i], *free[k])
                    th, tl = split_psum(xh[p][:, :, r * 128:(r + 1) * 128], xl[p][:, :, r * 128:(r + 1) * 128],
                                        bank[k][:].rearrange("p (c n) -> p c n", c=4), g, xh_free[p])
                    free[k] = [th, tl]
                a_ = dve(lambda e: e.tensor_tensor(pw[:], xs[p][:, :, 512:520],
                                                   ohE[:, i, :].unsqueeze(1).to_broadcast([128, 2, NE]), ALU.mult), xs_in[i])
                ww_t[i] = dve(lambda e: e.tensor_reduce(ww[p][:], pw[:], AX, ALU.add), a_, ww_free[p])
                xs_free[p] = [g, a_]
                x_ok[i] = (th, tl)

            a_ok = {}
            a_free = [None, None]
            ga_free = [None, None]
            up_free = [None, None]
            sg_free = [None, None]
            mn = [0]

            def gate_up(i, m):
                p = i % 2
                n = mn[0]
                mn[0] += 1
                k = n % 4
                q = n % 2
                def emit(e):
                    for h in range(2):
                        o = bank[k][:, h * 256:(h + 1) * 256]
                        for c in range(C):
                            off = (c % 2) * 1024 + h * 512 + m * 128
                            lh = wh[p][:, c // 2, off:off + 128]
                            ll = wl[p][:, c // 2, off:off + 128]
                            nc.tensor.matmul(o, lh, xh[p][:, c, :], start=(c == 0), stop=False)
                            nc.tensor.matmul(o, lh, xl[p][:, c, :], start=False, stop=False)
                            last_ = nc.tensor.matmul(o, ll, xh[p][:, c, :], start=False, stop=(c == C - 1))
                    return last_
                g = pe(emit, *x_ok[i], *w_ok[(i, 0)], *w_ok[(i, 1)], *free[k])
                if m == C - 1:
                    xh_free[p] = g
                tb = w_ok[(i, 2)][2]
                g_ = dve(lambda e: e.tensor_scalar(ga[q][:], bank[k][:, 0:256], gb[p][:, m:m + 1], LIMIT, ALU.add, ALU.min),
                         g, tb, ga_free[q])
                s_ = act(lambda e: e.activation(sg[q][:], ga[q][:], ACT.Sigmoid, scale=ALPHA), g_, sg_free[q])
                u_ = dve(lambda e: e.tensor_scalar(up[q][:], bank[k][:, 256:512], gb[p][:, 4 + m:5 + m], LIMIT, ALU.add,
                                                   ALU.min), up_free[q])
                free[k] = [u_]
                gb_free[p] = u_
                v_ = dve(lambda e: e.tensor_scalar(up[q][:], up[q][:], -LIMIT, 1.0, ALU.max, ALU.add), u_)
                y_ = dve(lambda e: e.tensor_tensor(up[q][:], up[q][:], ga[q][:], ALU.mult), v_)
                z_ = dve(lambda e: e.tensor_tensor(sg[q][:], up[q][:], sg[q][:], ALU.mult), y_, s_)
                h_ = act(lambda e: e.activation(ah[p][:, m, :], sg[q][:], ACT.Copy), z_, a_free[p])
                l_ = dve(lambda e: e.tensor_tensor(al[p][:, m, :], sg[q][:], ah[p][:, m, :].bitcast(F32), ALU.subtract), h_)
                ga_free[q] = z_
                up_free[q] = z_
                sg_free[q] = l_
                a_ok[i] = (h_, l_)

            ys_free = [None, None]
            add_t = [None]

            def down(i, r):
                p = i % 2
                k = 6 + r
                lh = [ah[p][:, c, r * 128:(r + 1) * 128] for c in range(C)]
                ll = [al[p][:, c, r * 128:(r + 1) * 128] for c in range(C)]
                rh = [wh[p][:, 2, c * D:(c + 1) * D] for c in range(C)]
                rl = [wl[p][:, 2, c * D:(c + 1) * D] for c in range(C)]
                g = pe(mm3(bank[k][:], lh, ll, rh, rl), *a_ok[i], *w_ok[(i, 2)], *free[k])
                a_ = act(lambda e: e.activation(ys[r][:], bank[k][:], ACT.Copy, scale=ww[p][:, r:r + 1]), g, ww_t[i], ys_free[r])
                free[k] = [a_]
                if r == 1:
                    wh_free[p] = g
                    a_free[p] = g
                    ww_free[p] = a_
                return a_

            def add_rows(i, toks):
                p = i % 2
                prev = add_t[0]
                for r in range(2):
                    z = dma("gpsimd", f"add{p}", lambda e, r=r: e.indirect_dma_start(
                        out, bass.IndirectOffsetOnAxis(ap=ti[:, 2 * i + r:2 * i + r + 1], axis=0), ys[r][:], None,
                        bounds_check=T - 1, oob_is_err=False, compute_op=ALU.add), toks[r], t_ti, *(prev or base_out))
                for r in range(2):
                    ys_free[r] = z
                add_t[0] = [z]

            fetch_x(0)
            for part in range(3):
                fetch_w(0, part)
            fetch_x(1)
            for part in range(3):
                split_expert(0, part)
            turn_x(0)
            for part in range(3):
                fetch_w(1, part)
            for i in range(NT + 1):
                if i < NT:
                    gate_up(i, 0)
                if i > 0:
                    toks = [down(i - 1, 0), down(i - 1, 1)]
                    add_rows(i - 1, toks)
                if i < NT:
                    if i + 1 < NT:
                        split_expert(i + 1, 0)
                        if i + 2 < NT:
                            fetch_w(i + 2, 0)
                    gate_up(i, 1)
                    if i + 1 < NT:
                        turn_x(i + 1)
                        if i + 2 < NT:
                            fetch_x(i + 2)
                        split_expert(i + 1, 1)
                        if i + 2 < NT:
                            fetch_w(i + 2, 1)
                    gate_up(i, 2)
                    if i + 1 < NT:
                        split_expert(i + 1, 2)
                        if i + 2 < NT:
                            fetch_w(i + 2, 2)
                    gate_up(i, 3)
            queues["sync"].append((None, [add_t[0][0]] + base_out[-2:], None, 0))

        block = top.enter_context(nc.Block())

        def drive(name):
            def body(e):
                seen = {}
                for fn, waits, sem, n in queues[name]:
                    for s, v in waits:
                        if seen.get(id(s), 0) < v:
                            e.wait_ge(s, v)
                            seen[id(s)] = v
                    if fn is not None:
                        fn(e).then_inc(sem, n)
            return body

        block.tensor(drive("tensor"))
        block.vector(drive("vector"))
        block.scalar(drive("scalar"))
        block.gpsimd(drive("gpsimd"))
        block.sync(drive("sync"))


def constants():
    p = np.arange(128)
    cst = np.zeros((2, 128, 128), np.float32)
    cst[0] = np.eye(128)
    cst[1] = p[:, None] < p[None, :]
    cm = np.zeros((128, 520), np.float32)
    cm[:, 0:32] = np.tile(np.arange(8), 4)
    cm[:, 32:40] = np.arange(8) * ER
    cm[:, 56] = p
    cm[:, 57] = (p < 8) | (p >= 16)
    cm[:, 58] = (p >= 8) & (p < 16)
    cm[:, 60] = p // 2
    cm[:, 61] = p
    i = np.arange(NT)
    cm[:, 136:136 + 8 * NT] = np.repeat(i, 8)
    cm[:, 320:320 + 8 * NT] = np.tile(np.arange(8), NT)
    cm[:, 504:520] = p[:, None] + 128 * np.arange(16)[None, :]
    return cst, cm


def kernel(**inputs):
    import concourse.bacc as _bacc
    from concourse import mybir as _mybir
    from concourse.bass_utils import run_bass_kernel_spmd as _run

    g = {k: np.asarray(v) for k, v in inputs.items()}
    a = "L0_xattn_"
    f = "L0_ffn_"
    cst, cm = constants()
    cm[:, 40:56] = np.tile(g[f + "router_bias"], 2)[None, :]
    gu = g[f + "gate_up_proj"].reshape(NE, C, 128, C, 128, 2).transpose(0, 2, 1, 5, 3, 4).reshape(NE * 128, C, 1024)
    dn = g[f + "down_proj"].reshape(NE, C, 128, D).transpose(0, 2, 1, 3).reshape(NE * 128, C * D)
    gbias = g[f + "gate_up_proj_bias"].reshape(NE, C, 128, 2).transpose(0, 2, 3, 1).reshape(NE * 128, 8)
    arrays = {
        "in_x": g["x"].reshape(T, D),
        "in_ctxT": g["ctx_2048"].transpose(0, 2, 1).reshape(B, C, 128, S).transpose(0, 2, 1, 3).reshape(B, 128, C * S),
        "in_w": np.stack([g[a + n].T.reshape(C, 128, D).transpose(1, 0, 2).reshape(128, C * D)
                          for n in ("w_q", "w_k_img", "w_v_img", "w_o")]),
        "in_bias": np.stack([np.broadcast_to(g[a + n], (128, D))
                             for n in ("b_q", "b_k_img", "b_v_img", "g_q", "g_k_img", "b_o")]),
        "in_bd3": np.concatenate([g[f + "down_proj_bias"]] * 3),
        "in_rwT": g[f + "router_weight"].T.reshape(C, 128, NE).transpose(1, 0, 2).reshape(128, C * NE),
        "in_wga": gu[:, 0:2].reshape(NE * 128, GW),
        "in_wgb": gu[:, 2:4].reshape(NE * 128, GW),
        "in_wd": np.concatenate([dn, gbias], axis=1),
        "in_cst": cst,
        "in_cm": cm,
    }
    arrays = {k: np.ascontiguousarray(v) for k, v in arrays.items()}
    nc = _bacc.Bacc("TRN2", target_bir_lowering=False, num_devices=1)
    args = [nc.dram_tensor(k, v.shape, _mybir.dt.from_np(v.dtype), kind="ExternalInput").ap() for k, v in arrays.items()]
    args.append(nc.dram_tensor("out_0", (T, D), _mybir.dt.float32, kind="ExternalOutput").ap())
    program(nc, *args)
    r = _run(nc, [arrays], core_ids=[0])
    return r.results[0]["out_0"].reshape(B, S, D)
```

```python
from contextlib import ExitStack

import numpy as np

import concourse.bass as bass
from concourse import mybir

F32 = mybir.dt.float32
F32R = mybir.dt.float32r
BF16 = mybir.dt.bfloat16
U32 = mybir.dt.uint32
I32 = mybir.dt.int32
ALU = mybir.AluOpType
ACT = mybir.ActivationFunctionType
AX = mybir.AxisListType.X

B = 8
S = 256
D = 512
NH = 16
HD = 32
C = 4
NE = 8
T = 2048
LN_EPS = 1e-5
RMS_EPS = 1e-6
SCALE = 1.0 / float(np.sqrt(np.float32(HD)))
ALPHA = 1.702
LIMIT = 7.0
NT = 23
ER = 2048
RW = 520
SKIP = 4096
TR = NE * ER // 128
GW = 2048
DW = 2056


def program(nc, x, ctxT, wqkvo, bias, bd3, rwT, wga, wgb, wd, cst, cm, out):
    qs = [nc.dram_tensor(f"qs{b}", (2, HD, NH * S), F32, kind="Internal").ap() for b in range(B)]
    ks = [nc.dram_tensor(f"ks{b}", (2, HD, NH * S), F32, kind="Internal").ap() for b in range(B)]
    vs = [nc.dram_tensor(f"vs{b}", (128, 2 * D), F32, kind="Internal").ap() for b in range(B)]
    hb = nc.dram_tensor("hb", (T, RW), F32, kind="Internal").ap()
    slot = nc.dram_tensor("slot", ((TR + 1) * 128, 1), F32, kind="Internal").ap()

    with ExitStack() as top:
        queues = {n: [] for n in ("tensor", "vector", "scalar", "gpsimd", "sync")}
        done = {n: top.enter_context(nc.semaphore(f"done_{n}")) for n in ("tensor", "vector", "scalar", "gpsimd")}
        count = {n: 0 for n in done}
        dsem = {}
        dcount = {}

        def op(eng, fn, *waits):
            count[eng] += 1
            queues[eng].append((fn, [w for w in waits if w is not None], done[eng], 1))
            return (done[eng], count[eng])

        def pe(fn, *waits):
            return op("tensor", fn, *waits)

        def dve(fn, *waits):
            return op("vector", fn, *waits)

        def act(fn, *waits):
            return op("scalar", fn, *waits)

        def pool(fn, *waits):
            return op("gpsimd", fn, *waits)

        def dma(eng, key, fn, *waits):
            if key not in dsem:
                dsem[key] = top.enter_context(nc.semaphore(f"d_{key}"))
                dcount[key] = 0
            dcount[key] += 16
            queues[eng].append((fn, [w for w in waits if w is not None], dsem[key], 16))
            return (dsem[key], dcount[key])

        def load(key, dst, src, *waits, eng="sync"):
            return dma(eng, key, lambda e: e.dma_start(dst, src), *waits)

        def sb(ctx, name, shape, dt=F32):
            return ctx.enter_context(nc.sbuf_tensor(name, shape, dt))

        bank = [top.enter_context(nc.psum_tensor(f"bank{i}", [128, 512], F32)) for i in range(8)]
        free = [[] for _ in range(8)]

        ident = sb(top, "ident", [128, 128])
        cstt = sb(top, "cstt", [128, 256])
        tri = sb(top, "tri", [128, 128], BF16)
        ones = sb(top, "ones", [128, 128], BF16)
        onef = sb(top, "onef", [128, 32])
        cmt = sb(top, "cmt", [128, cm.shape[1]])
        half = sb(top, "half", [128, 2])
        run = sb(top, "run", [128, NE])
        rw = sb(top, "rw", [128, C * NE])
        t_id = load("cst", ident[:], cst[0])
        t_cm = load("cm", cmt[:], cm)
        t_tr = load("tri", cstt[:, 0:128], cst[1])
        t_rw = load("rw", rw[:], rwT)
        t_tri = dve(lambda e: e.tensor_copy(tri[:], cstt[:, 0:128]), t_tr)
        t_ones = dve(lambda e: e.memset(ones[:], 1.0))
        t_onef = dve(lambda e: e.memset(onef[:], 1.0))
        t_half = dve(lambda e: e.memset(half[:], -0.5))
        IOTA = cmt[:, 0:32].rearrange("p (t j e) -> p t j e", t=2, j=2)
        IO8 = cmt[:, 0:8]
        EBASE = cmt[:, 32:40]
        RB = cmt[:, 40:56]
        PIDX = cmt[:, 56:57]
        MH = cmt[0:24, 57:58]
        ML = cmt[0:24, 58:59]
        TI8 = cmt[:, 136:136 + 8 * NT].rearrange("p (i e) -> p i e", e=8)
        IT8 = cmt[:, 320:320 + 8 * NT].rearrange("p (i e) -> p i e", e=8)
        TOK = cmt[:, 504:520]
        SPT = cmt[:, 60:61]
        SPR = cmt[:, 61:62]
        skips = sb(top, "skips", [128, TR + 1])
        t_skip = pool(lambda e: e.memset(skips[:], float(SKIP)))
        t_slot = load("slot", slot.rearrange("(p n) o -> p (n o)", p=128), skips[:], t_skip)
        t_run = dve(lambda e: e.tensor_copy(run[:], EBASE), t_cm)

        def mm3(o, lh, ll, rh, rl):
            def emit(e):
                n = len(lh)
                last = None
                for c in range(n):
                    for j, (a, b) in enumerate(((lh[c], rh[c]), (lh[c], rl[c]), (ll[c], rh[c]))):
                        last = nc.tensor.matmul(o, a, b, start=(c == 0 and j == 0), stop=(c == n - 1 and j == 2))
                return last
            return emit

        def transposes(o, src, n, np_=128, w=128):
            def emit(e):
                for k in range(n):
                    last = nc.tensor.transpose(o[:, k * np_:(k + 1) * np_], src[:, k * w:(k + 1) * w],
                                               ident[0:np_, 0:np_])
                return last
            return emit

        def split_psum(hi, lo, src, ready, *waits):
            th = act(lambda e: e.activation(hi, src, ACT.Copy), ready, *waits)
            tl = dve(lambda e: e.tensor_tensor(lo, src, hi.bitcast(F32), ALU.subtract), th)
            return th, tl

        v_out = [None] * B
        q_out = [None] * B
        k_out = [None] * B
        wo_ctx = ExitStack()
        whi3 = sb(wo_ctx, "wohi", [128, C * D], F32R)
        wlo3 = sb(wo_ctx, "wolo", [128, C * D], F32R)
        bo = sb(wo_ctx, "bo", [128, D])
        bdh = sb(wo_ctx, "bdh", [24, D], F32R)
        bds = sb(wo_ctx, "bds", [24, D], F32R)
        with ExitStack() as ctx:
            WH = [sb(ctx, f"wh{i}", [128, C * D], F32R) for i in range(3)] + [whi3]
            WL = [sb(ctx, f"wl{i}", [128, C * D], F32R) for i in range(3)] + [wlo3]
            wraw = [sb(ctx, f"wraw{i}", [128, C * D]) for i in range(2)]
            bi = [sb(ctx, f"bi{i}", [128, D]) for i in range(5)]
            bdr = sb(ctx, "bdr", [24, D])
            bdl = sb(ctx, "bdl", [24, D])
            xt = [sb(ctx, f"xt{i}", [128, 2, D]) for i in range(2)]
            st6 = sb(ctx, "st6", [128, 2, 6])
            mv = sb(ctx, "mv", [128, 2, 2])
            ve = sb(ctx, "ve", [128, 2])
            rs = sb(ctx, "rs", [128, 2])
            hn = [sb(ctx, f"hn{i}", [128, D]) for i in range(2)]
            hth = [sb(ctx, f"hth{i}", [128, C, S], F32R) for i in range(2)]
            htl = [sb(ctx, f"htl{i}", [128, C, S], F32R) for i in range(2)]
            cr = [sb(ctx, f"cr{i}", [128, C * S]) for i in range(2)]
            cth = [sb(ctx, f"cth{i}", [128, C * S], F32R) for i in range(2)]
            ctl = [sb(ctx, f"ctl{i}", [128, C * S], F32R) for i in range(2)]
            pf = [sb(ctx, f"pf{i}", [128, D]) for i in range(4)]
            sqj = sb(ctx, "sqj", [128, D])
            ss = [sb(ctx, f"ss{i}", [128, 1]) for i in range(4)]
            sr = [sb(ctx, f"sr{i}", [128, 1]) for i in range(4)]
            qth = [sb(ctx, f"qth{i}", [128, C, S], F32R) for i in range(2)]
            qtl = [sb(ctx, f"qtl{i}", [128, C, S], F32R) for i in range(2)]
            vt = [sb(ctx, f"vt{i}", [128, 2 * D]) for i in range(2)]

            x_in = {}
            x_free = [None, None]
            c_in = {}
            c_free = [[], []]
            ht_free = [None, None]
            ct_free = [None, None]
            hn_free = [None, None]

            def load_batch(b):
                p = b % 2
                x_in[b] = load(f"x{p}", xt[p][:], x[b * S:(b + 1) * S, :].rearrange("(t p) d -> p t d", p=128), x_free[p])
                c_in[b] = load(f"c{p}", cr[p][:], ctxT[b], *c_free[p])

            load_batch(0)
            b_in = None
            w_t = {}

            def load_w(i, p, *waits):
                return load(f"w{p}", wraw[p][:], wqkvo[i], *waits)

            def split_w(i, p, ready):
                th = act(lambda e: e.activation(WH[i][:], wraw[p][:], ACT.Copy), ready)
                tl = dve(lambda e: e.tensor_tensor(WL[i][:], wraw[p][:], WH[i][:].bitcast(F32), ALU.subtract), th)
                w_t[i] = (th, tl)
                return tl

            w0 = load_w(0, 0)
            w1 = load_w(1, 1)
            for i, dst in enumerate(bi):
                b_in = load("bi", dst[:], bias[i])
            b_in = load("bi", bo[:], bias[5])
            t_bd = load("bd", bdr[:], bd3)
            load_batch(1)

            ht_t = {}
            ct_t = {}
            ring = {"m": 0, "t": 0}

            def mbank():
                ring["m"] += 1
                return (ring["m"] - 1) % 4

            def tbank():
                ring["t"] += 1
                return 4 + (ring["t"] - 1) % 4

            def layer_norm(b):
                p = b % 2
                for t in range(2):
                    s_ = dve(lambda e, t=t: e.bn_stats(st6[:, t, :], xt[p][:, t, :]), x_in[b], ln_free[0])
                for t in range(2):
                    a_ = dve(lambda e, t=t: e.bn_aggr(mv[:, t, :], st6[:, t, :]), s_)
                v_ = dve(lambda e: e.tensor_scalar(ve[:], mv[:, :, 1], LN_EPS, None, ALU.add), a_)
                r_ = pool(lambda e: e.tensor_tensor(rs[:], ve[:], half[:], ALU.pow), v_, t_half)
                for t in range(2):
                    n_ = dve(lambda e, t=t: e.tensor_scalar(hn[t][:], xt[p][:, t, :], mv[:, t, 0:1], rs[:, t:t + 1],
                                                            ALU.subtract, ALU.mult), r_, hn_free[t])
                    ln_t[(b, t)] = n_
                ln_free[0] = n_
                x_free[p] = n_

            ln_free = [None]
            ln_t = {}

            def ln_transposes(b):
                p = b % 2
                for t in range(2):
                    k = tbank()
                    g = pe(transposes(bank[k], hn[t], 4), ln_t[(b, t)], t_id, *free[k])
                    hn_free[t] = g
                    src = bank[k][:].rearrange("p (c n) -> p c n", c=4)
                    th, tl = split_psum(hth[p][:, :, t * 128:(t + 1) * 128], htl[p][:, :, t * 128:(t + 1) * 128],
                                        src, g, ht_free[p])
                    free[k] = [th, tl]
                ht_t[b] = (th, tl)

            def ctx_split(b):
                p = b % 2
                th = act(lambda e: e.activation(cth[p][:], cr[p][:], ACT.Copy), c_in[b], ct_free[p])
                tl = dve(lambda e: e.tensor_tensor(ctl[p][:], cr[p][:], cth[p][:].bitcast(F32), ALU.subtract), th)
                ct_t[b] = (th, tl)
                c_free[p] = [th, tl]

            layer_norm(0)
            ctx_split(0)
            r0 = split_w(0, 0, w0)
            w2 = load_w(2, 0, r0)
            r1 = split_w(1, 1, w1)
            w3 = load_w(3, 1, r1)
            ln_transposes(0)
            r2 = split_w(2, 0, w2)
            later = [lambda: split_w(3, 1, w3)]

            def bd_split():
                th = act(lambda e: e.activation(bdh[:], bdr[:], ACT.Copy), t_bd)
                tl = dve(lambda e: e.tensor_tensor(bdl[:], bdr[:], bdh[:].bitcast(F32), ALU.subtract), th)
                tm = dve(lambda e: e.tensor_scalar(bdl[:], bdl[:], ML, None, ALU.mult), tl, t_cm)
                return dve(lambda e: e.scalar_tensor_tensor(out=bds[:], in0=bdh[:].bitcast(F32), scalar=MH, in1=bdl[:],
                                                            op0=ALU.mult, op1=ALU.add), tm)

            pf_free = [None] * 4
            qt_free = [None, None]
            vt_free = [None, None]
            units = 0

            def project(b, kind, t):
                nonlocal units
                p = b % 2
                k = mbank()
                if kind == 0:
                    lh = [hth[p][:, c, t * 128:(t + 1) * 128] for c in range(C)]
                    ll = [htl[p][:, c, t * 128:(t + 1) * 128] for c in range(C)]
                    ready = ht_t[b]
                else:
                    lh = [cth[p][:, c * S + t * 128:c * S + (t + 1) * 128] for c in range(C)]
                    ll = [ctl[p][:, c * S + t * 128:c * S + (t + 1) * 128] for c in range(C)]
                    ready = ct_t[b]
                rh = [WH[kind][:, c * D:(c + 1) * D] for c in range(C)]
                rl = [WL[kind][:, c * D:(c + 1) * D] for c in range(C)]
                g = pe(mm3(bank[k][:], lh, ll, rh, rl), *ready, *w_t[kind], *free[k])
                if kind == 2:
                    a = dve(lambda e: e.tensor_tensor(vt[p][:, t * D:(t + 1) * D], bank[k][:], bi[2][:], ALU.add),
                            g, b_in, vt_free[p])
                    free[k] = [a]
                    return g, a
                u = units % 4
                units += 1
                a = dve(lambda e: e.tensor_tensor(pf[u][:], bank[k][:], bi[kind][:], ALU.add), g, b_in, pf_free[u])
                free[k] = [a]
                s_ = act(lambda e: e.activation(sqj[:], pf[u][:], ACT.Square, accum_out=ss[u][:]), a)
                m_ = dve(lambda e: e.tensor_scalar(ss[u][:], ss[u][:], 1.0 / D, RMS_EPS, ALU.mult, ALU.add), s_)
                r_ = pool(lambda e: e.tensor_tensor(sr[u][:], ss[u][:], half[:, 0:1], ALU.pow), m_, t_half)
                return g, (u, r_)

            def normalise(kind, u, r_):
                return dve(lambda e: e.scalar_tensor_tensor(out=pf[u][:], in0=pf[u][:], scalar=sr[u][:, 0:1],
                                                            in1=bi[3 + kind][:], op0=ALU.mult, op1=ALU.mult), r_)

            def to_heads(b, kind, t, u, n_):
                k = tbank()
                g = pe(transposes(bank[k], pf[u], 4), n_, *free[k])
                pf_free[u] = g
                src = bank[k][:].rearrange("p (c n) -> p c n", c=4)
                th, tl = split_psum(qth[kind][:, :, t * 128:(t + 1) * 128], qtl[kind][:, :, t * 128:(t + 1) * 128],
                                    src, g, qt_free[kind])
                free[k] = [th, tl]
                return th, tl

            def store_heads(b, kind, th, tl):
                dst = (qs if kind == 0 else ks)[b]
                for n, (tile, tok) in enumerate(((qth[kind], th), (qtl[kind], tl))):
                    for h4 in range(4):
                        o = dst[n].rearrange("d (h m) -> d h m", h=4)[:, h4, :]
                        i = tile[32 * h4:32 * h4 + 32, :, :].bitcast(F32).rearrange("p c n -> p (c n)")
                        z = load(f"s{kind}", o, i, tok)
                qt_free[kind] = z
                (q_out if kind == 0 else k_out)[b] = z

            for b in range(B):
                p = b % 2
                if 0 < b and b + 1 < B:
                    load_batch(b + 1)
                _, q0 = project(b, 0, 0)
                _, k0 = project(b, 1, 0)
                nq0 = normalise(0, *q0)
                if b + 1 < B:
                    layer_norm(b + 1)
                _, _ = project(b, 2, 0)
                nk0 = normalise(1, *k0)
                to_heads(b, 0, 0, q0[0], nq0)
                gq, q1 = project(b, 0, 1)
                ht_free[p] = gq
                to_heads(b, 1, 0, k0[0], nk0)
                _, k1 = project(b, 1, 1)
                nq1 = normalise(0, *q1)
                if b + 1 < B:
                    ln_transposes(b + 1)
                gv, vv = project(b, 2, 1)
                ct_free[p] = gv
                vt_free[p] = v_out[b] = load(f"v{p}", vs[b], vt[p][:], vv)
                nk1 = normalise(1, *k1)
                store_heads(b, 0, *to_heads(b, 0, 1, q1[0], nq1))
                if b + 1 < B:
                    ctx_split(b + 1)
                store_heads(b, 1, *to_heads(b, 1, 1, k1[0], nk1))
                if b == 0:
                    later[0]()
                    t_bds = bd_split()
            over_a = [(done[n], count[n]) for n in ("tensor", "vector", "scalar", "gpsimd")] + \
                     [(dsem[k], dcount[k]) for k in ("s0", "s1", "v0", "v1")]

        with ExitStack() as ctx:
            qst = [sb(ctx, f"qst{i}", [128, NH, S], F32R) for i in range(3)]
            kst = [sb(ctx, f"kst{i}", [128, NH, S], F32R) for i in range(3)]
            vb = [sb(ctx, f"vb{i}", [128, 2 * D]) for i in range(3)]
            mx = [sb(ctx, f"mx{i}", [128, 2, NH]) for i in range(2)]
            nm = [sb(ctx, f"nm{i}", [8, 2, 128]) for i in range(2)]
            pt = [sb(ctx, f"pt{i}", [128, 512]) for i in range(6)]
            rec = [sb(ctx, f"rec{i}", [128, S]) for i in range(1)]
            of = [sb(ctx, f"of{i}", [128, S]) for i in range(2)]
            oh_ = [sb(ctx, f"oh{i}", [128, C, S], F32R) for i in range(2)]
            ol_ = [sb(ctx, f"ol{i}", [128, C, S], F32R) for i in range(1)]
            xb = [sb(ctx, f"xb{i}", [128, D]) for i in range(2)]
            hr = [sb(ctx, f"hr{i}", [128, RW]) for i in range(2)]
            h2t = sb(ctx, "h2t", [128, 512])
            st6B = sb(ctx, "st6b", [128, 6])
            mvB = sb(ctx, "mvb", [128, 2])
            veB = sb(ctx, "veb", [128, 1])
            rsB = sb(ctx, "rsb", [128, 1])
            nmB = sb(ctx, "nmb", [128, 1])
            nm_free = [None]
            lg = sb(ctx, "lg", [128, 2, NE])
            m8 = sb(ctx, "m8", [128, 2, 8])
            ix = sb(ctx, "ix", [128, 2, 8], U32)
            ixf = sb(ctx, "ixf", [128, 2, 8])
            oht = sb(ctx, "oht", [128, 2, 2, NE])
            dd = sb(ctx, "dd", [128, 2])
            ee = sb(ctx, "ee", [128, 2])
            se = sb(ctx, "se", [128, 2])
            wa = sb(ctx, "wa", [128, 2])
            wb = sb(ctx, "wb", [128, 2])
            tmp8 = sb(ctx, "tmp8", [128, 2, NE])
            M = sb(ctx, "M", [128, 2, NE], BF16)
            pos = sb(ctx, "pos", [128, 2, NE])
            pr = sb(ctx, "pr", [128, 2, 2, NE])
            sl = sb(ctx, "sl", [128, 4])
            si = [sb(ctx, f"si{i}", [128, 4], U32) for i in range(2)]
            sc3 = sb(ctx, "sc3", [128, 2, 3, NE])
            s3t = sb(ctx, "s3t", [24, 256], F32R)
            ob = [sb(ctx, f"ob{i}", [128, D]) for i in range(2)]

            st_in = {}
            st_free = [over_a, over_a, over_a]
            v_in = {}
            one_t = []
            for i in range(3):
                one_t.append(dve(lambda e, i=i: e.memset(kst[i][96:97, :, :].bitcast(F32), 1.0), *(over_a if i == 0 else ())))

            def load_stacks(b):
                i = b % 3
                w = list(st_free[i])
                for n, (dst, src, tok, part) in enumerate(((qst, qs, q_out, (0, 0, 1)), (kst, ks, k_out, (0, 1, 0)))):
                    for quad, plane in enumerate(part):
                        st_in[b] = load(f"st{i}", dst[i][32 * quad:32 * quad + 32, :, :].bitcast(F32)
                                        .rearrange("p h n -> p (h n)"), src[b][plane], tok[b], *w)
                v_in[b] = load(f"vb{i}", vb[i][:], vs[b], v_out[b], *w)

            mx_t = {}
            nm_t = {}
            m_in = {}
            mx_free = [over_a, over_a]

            def head(b, cb, h4):
                return h4 * 4 + cb

            def score_max(b, n):
                cb, h4 = divmod(n, 4)
                s_ = head(b, cb, h4)
                i = b % 3
                k = n % 2
                def emit(e):
                    for t in range(2):
                        last = nc.tensor.matmul(bank[k][:, t * 256:(t + 1) * 256],
                                                qst[i][0:96, s_, t * 128:(t + 1) * 128], kst[i][0:96, s_, :],
                                                start=True, stop=True)
                    return last
                g = pe(emit, st_in[b], *free[k])
                d_ = dve(lambda e: e.tensor_reduce(mx[b % 2][:, :, n], bank[k][:].rearrange("p (t n) -> p t n", t=2),
                                                   AX, ALU.max), g, *mx_free[b % 2])
                free[k] = [d_]
                mx_t[(b, n // 8)] = d_

            def send_max(b, half_):
                k = 7
                def emit(e):
                    for t in range(2):
                        last = nc.tensor.transpose(bank[k][0:8, t * 128:(t + 1) * 128],
                                                   mx[b % 2][:, t, 8 * half_:8 * half_ + 8], ident[:])
                    return last
                g = pe(emit, mx_t[(b, half_)], *free[k])
                if half_:
                    mx_free[b % 2] = [g]
                a_ = act(lambda e: e.activation(nm[half_][:].rearrange("h t n -> h (t n)"), bank[k][0:8, 0:256],
                                                ACT.Copy, scale=-1.0), g, m_in.get((b - 1, half_)))
                free[k] = [a_]
                row = qst[b % 3][96:97, :, :].bitcast(F32).rearrange("p (h c) n -> p c h n", c=4)
                for j in range(2):
                    m_in[(b, half_)] = load(f"m{half_}", row[:, 2 * half_ + j, :, :],
                                            nm[half_][4 * j:4 * j + 4, :, :].rearrange("h t n -> h (t n)"), a_)

            pt_free = [None] * 6
            pt_t = {}
            pn = [0]

            def probs(b, n):
                cb, h4 = divmod(n, 4)
                s_ = head(b, cb, h4)
                i = b % 3
                k = 2 + n % 2
                u = pn[0] % 6
                pn[0] += 1
                def emit(e):
                    for t in range(2):
                        last = nc.tensor.matmul(bank[k][:, t * 256:(t + 1) * 256],
                                                kst[i][0:97, s_, t * 128:(t + 1) * 128], qst[i][0:97, s_, :],
                                                start=True, stop=True)
                    return last
                g = pe(emit, st_in[b], m_in[(b, n // 8)], one_t[2], *free[k])
                a_ = act(lambda e: e.activation(pt[u][:], bank[k][:], ACT.Exp, scale=SCALE), g, pt_free[u])
                free[k] = [a_]
                pt_t[(b, n)] = (u, a_)
                return g

            o_t = {}
            of_free = [None, None]
            o_free = [None, None]
            gn = [0]

            def values(b, g4):
                k = 4 + gn[0] % 2
                f = gn[0] % 2
                gn[0] += 1
                us = [pt_t[(b, 4 * g4 + j)] for j in range(4)]
                def emit(e):
                    for half_ in range(2):
                        for t in range(2):
                            for j in range(4):
                                lhs = onef[:] if half_ else vb[b % 3][:, t * D + g4 * 128 + 32 * j:t * D + g4 * 128 + 32 * j + 32]
                                last = nc.tensor.matmul(bank[k][32 * j:32 * j + 32, half_ * 256:half_ * 256 + 256], lhs,
                                                        pt[us[j][0]][:, t * 256:(t + 1) * 256],
                                                        start=(t == 0), stop=(t == 1))
                    return last
                g = pe(emit, *[u[1] for u in us], v_in[b], t_onef, *free[k])
                for u in us:
                    pt_free[u[0]] = g
                r_ = dve(lambda e: e.reciprocal(rec[0][:], bank[k][:, 256:512]), g)
                m_ = dve(lambda e: e.tensor_tensor(of[f][:], bank[k][:, 0:256], rec[0][:], ALU.mult), r_, of_free[f])
                free[k] = [m_]
                h_ = act(lambda e: e.activation(oh_[b % 2][:, g4, :], of[f][:], ACT.Copy), m_, o_free[b % 2])
                l_ = pool(lambda e: e.tensor_tensor(ol_[0][:, g4, :], of[f][:], oh_[b % 2][:, g4, :].bitcast(F32),
                                                    ALU.subtract), h_, o_free[(b + 1) % 2])
                of_free[f] = l_
                o_t[b] = (h_, l_)
                return g

            xb_free = [None, None]
            xb_in = {}
            hr_free = [None, None]
            x2_t = {}
            h2_t = {}
            ob_free = [None, None]
            base_out = []
            lg_t = {}

            def load_x(b):
                for t in range(2):
                    xb_in[(b, t)] = load(f"xb{t}", xb[t][:], x[b * S + t * 128:b * S + (t + 1) * 128, :], xb_free[t],
                                         *(over_a if b == 0 else ()))

            def out_project(b, t):
                k = 6 + t
                lh = [oh_[b % 2][:, c, t * 128:(t + 1) * 128] for c in range(C)]
                ll = [ol_[0][:, c, t * 128:(t + 1) * 128] for c in range(C)]
                rh = [whi3[:, c * D:(c + 1) * D] for c in range(C)]
                rl = [wlo3[:, c * D:(c + 1) * D] for c in range(C)]
                g = pe(mm3(bank[k][:], lh, ll, rh, rl), *o_t[b], *w_t[3], *free[k])
                if t == 1:
                    o_free[b % 2] = g
                p_ = pool(lambda e: e.tensor_tensor(xb[t][:], xb[t][:], bo[:], ALU.add), xb_in[(b, t)], b_in)
                a_ = dve(lambda e: e.tensor_tensor(xb[t][:], bank[k][:], xb[t][:], ALU.add), g, p_)
                free[k] = [a_]
                s_ = dve(lambda e: e.bn_stats(st6B[:], xb[t][:]), a_)
                s_ = dve(lambda e: e.bn_aggr(mvB[:], st6B[:]), s_)
                v_ = dve(lambda e: e.tensor_scalar(veB[:], mvB[:, 1:2], LN_EPS, None, ALU.add), s_)
                r_ = pool(lambda e: e.tensor_tensor(rsB[:], veB[:], half[:, 0:1], ALU.pow), v_, nm_free[0])
                n_ = dve(lambda e: e.tensor_scalar(nmB[:], mvB[:, 0:1], rsB[:, 0:1], -1.0, ALU.mult, ALU.mult), r_, nm_free[0])
                h_ = act(lambda e: e.activation(hr[t][:, 0:512], xb[t][:], ACT.Identity, scale=rsB[:, 0:1],
                                                bias=nmB[:, 0:1]), n_, hr_free[t])
                nm_free[0] = h_
                x2_t[(b, t)] = a_
                h2_t[(b, t)] = h_

            h2t_free = [None]

            def router_turn(b, t):
                k = 7
                g = pe(transposes(bank[k], hr[t], 4), h2_t[(b, t)], *free[k])
                a_ = act(lambda e: e.activation(h2t[:], bank[k][:], ACT.Copy), g, h2t_free[0])
                free[k] = [a_]
                h2t_t[0] = a_

            h2t_t = [None]

            def router(b, t):
                k = 6
                def emit(e):
                    for c in range(C):
                        last = nc.tensor.matmul(bank[k][:, t * 8:t * 8 + 8], h2t[:, c * 128:(c + 1) * 128],
                                                rw[:, c * NE:(c + 1) * NE], start=(c == 0), stop=(c == C - 1))
                    return last
                g = pe(emit, h2t_t[0], t_rw, *free[k])
                h2t_free[0] = g
                free[k] = [g]
                lg_t[(b, t)] = g

            rk = [None]
            si_free = [None, None]
            pass

            def choose(b):
                k2 = 6
                c_ = dve(lambda e: e.tensor_tensor(lg[:].rearrange("p t e -> p (t e)"), bank[k2][:, 0:16], RB, ALU.add),
                         lg_t[(b, 0)], lg_t[(b, 1)])
                free[k2] = [c_]
                for t in range(2):
                    m_ = dve(lambda e, t=t: e.max(m8[:, t, :], lg[:, t, :]), c_)
                d_ = dve(lambda e: e.tensor_tensor(dd[:], m8[:, :, 1], m8[:, :, 0], ALU.subtract), m_)
                e_ = act(lambda e: e.activation(ee[:], dd[:], ACT.Exp), d_)
                for t in range(2):
                    i_ = dve(lambda e, t=t: e.max_index(ix[:, t, :], m8[:, t, :], lg[:, t, :]), m_)
                f_ = dve(lambda e: e.tensor_copy(ixf[:], ix[:]), i_)
                o_ = dve(lambda e: e.tensor_tensor(oht[:], IOTA, ixf[:, :, 0:2].unsqueeze(3).to_broadcast([128, 2, 2, NE]),
                                                   ALU.is_equal), f_)
                M_ = dve(lambda e: e.tensor_tensor(M[:], oht[:, :, 0, :], oht[:, :, 1, :], ALU.add), o_, rk[0])
                s_ = dve(lambda e: e.tensor_scalar(se[:], ee[:], 1.0, None, ALU.add), e_)
                w_ = dve(lambda e: e.reciprocal(wa[:], se[:]), s_)
                w2_ = dve(lambda e: e.tensor_tensor(wb[:], ee[:], wa[:], ALU.mult), w_)
                for t in range(2):
                    a_ = dve(lambda e, t=t: e.tensor_scalar(tmp8[:, t, :], oht[:, t, 0, :], wa[:, t:t + 1], None, ALU.mult), w_)
                for t in range(2):
                    y_ = dve(lambda e, t=t: e.scalar_tensor_tensor(out=hr[t][:, 512:520], in0=oht[:, t, 1, :],
                                                                   scalar=wb[:, t:t + 1], in1=tmp8[:, t, :],
                                                                   op0=ALU.mult, op1=ALU.add), a_, w2_, *([hr_free[t]]))
                for t in range(2):
                    z_ = dve(lambda e, t=t: e.tensor_copy(sc3[:, t, 0, :].bitcast(F32R), hr[t][:, 512:520]), y_, s3_free[0])
                for t in range(2):
                    z1 = dve(lambda e, t=t: e.tensor_copy(sc3[:, t, 1, :], sc3[:, t, 0, :]), z_)
                    z2 = dve(lambda e, t=t: e.tensor_tensor(sc3[:, t, 2, :], hr[t][:, 512:520], sc3[:, t, 0, :], ALU.subtract), z_)
                return M_, y_, z2

            s3_free = [None]
            s3t_free = [None]

            def rank(b, M_, y_, z2):
                k = 7
                def emit(e):
                    r = bank[k]
                    nc.tensor.matmul(r[:, 0:8], tri[:], M[:, 0, :], start=True, stop=True)
                    nc.tensor.matmul(r[:, 8:16], tri[:], M[:, 1, :], start=True, stop=False)
                    nc.tensor.matmul(r[:, 8:16], ones[:], M[:, 0, :], start=False, stop=True)
                    nc.tensor.matmul(r[:, 16:24], ones[:], M[:, 0, :], start=True, stop=False)
                    return nc.tensor.matmul(r[:, 16:24], ones[:], M[:, 1, :], start=False, stop=True)
                g = pe(emit, M_, t_tri, t_ones, *free[k])
                rk[0] = g
                p_ = dve(lambda e: e.tensor_tensor(pos[:], bank[k][:, 0:16].rearrange("p (t e) -> p t e", t=2),
                                                   run[:].unsqueeze(1).to_broadcast([128, 2, NE]), ALU.add), g, t_run, run_t[0])
                n_ = dve(lambda e: e.tensor_tensor(run[:], bank[k][:, 16:24], run[:], ALU.add), p_)
                run_t[0] = n_
                free[k] = [n_]
                q_ = dve(lambda e: e.tensor_tensor(pr[:], oht[:], pos[:].unsqueeze(2).to_broadcast([128, 2, 2, NE]), ALU.mult), p_)
                r_ = dve(lambda e: e.tensor_reduce(sl[:], pr[:].rearrange("p t j e -> p (t j) e"), AX, ALU.add), q_)
                i_ = dve(lambda e: e.tensor_copy(si[b % 2][:], sl[:]), r_, si_free[b % 2])
                for t in range(2):
                    for j in range(2):
                        n = 2 * t + j
                        z = dma("gpsimd", f"sc{b % 2}", lambda e, n=n, t=t: e.indirect_dma_start(
                            slot, bass.IndirectOffsetOnAxis(ap=si[b % 2][:, n:n + 1], axis=0),
                            TOK[:, 2 * b + t:2 * b + t + 1], None), i_, t_slot)
                    hr_free[t] = load(f"hr{t}", hb[b * S + t * 128:b * S + (t + 1) * 128, :], hr[t][:], y_)
                si_free[b % 2] = z

            run_t = [None]

            def add_bias(b, z2):
                k = 6
                def emit(e):
                    for t in range(2):
                        last = nc.tensor.transpose(bank[k][0:24, t * 128:(t + 1) * 128],
                                                   sc3[:, t, :, :].rearrange("p a e -> p (a e)"), ident[:])
                    return last
                g = pe(emit, z2, *free[k])
                s3_free[0] = g
                a_ = act(lambda e: e.activation(s3t[:], bank[k][0:24, 0:256], ACT.Copy), g, s3t_free[0])
                free[k] = [a_]
                for t in range(2):
                    k = 7 - t
                    g = pe(lambda e, t=t, k=k: nc.tensor.matmul(bank[k][:], s3t[:, t * 128:(t + 1) * 128], bds[:],
                                                                start=True, stop=True), a_, t_bds, *free[k])
                    d_ = dve(lambda e, t=t, k=k: e.tensor_tensor(ob[t][:], bank[k][:], xb[t][:], ALU.add), g, ob_free[t])
                    free[k] = [d_]
                    xb_free[t] = d_
                    ob_free[t] = load(f"ob{t}", out[b * S + t * 128:b * S + (t + 1) * 128, :], ob[t][:], d_)
                s3t_free[0] = g
                base_out.append(ob_free[0])
                base_out.append(ob_free[1])

            load_stacks(0)
            load_x(0)
            load_stacks(1)
            load_stacks(2)
            for step in range(-1, B + 1):
                bB, bC, bD = step + 1, step, step - 1
                for n in range(NH):
                    if bB < B:
                        score_max(bB, n)
                        if n == 9:
                            send_max(bB, 0)
                    if 0 <= bC < B:
                        probs(bC, n)
                        if n == 1:
                            send_max(bC, 1)
                    if 0 <= bD:
                        if n == 1:
                            gv = values(bD, 3)
                            if bD + 3 < B:
                                st_free[bD % 3] = [gv]
                                load_stacks(bD + 3)
                        elif n == 4:
                            out_project(bD, 0)
                        elif n == 5:
                            out_project(bD, 1)
                        elif n == 7:
                            router_turn(bD, 0)
                        elif n == 8:
                            router(bD, 0)
                            router_turn(bD, 1)
                        elif n == 10:
                            router(bD, 1)
                            M_, y_, z2 = choose(bD)
                        elif n == 12:
                            rank(bD, M_, y_, z2)
                        elif n == 14:
                            add_bias(bD, z2)
                            if bD + 1 < B:
                                load_x(bD + 1)
                    if 0 <= bC < B and n >= 5 and n % 4 == 1:
                        values(bC, n // 4 - 1)
            over_b = [(done[n], count[n]) for n in ("tensor", "vector", "scalar", "gpsimd")] + base_out[-2:] + \
                     [(dsem[k], dcount[k]) for k in ("sc0", "sc1", "hr0", "hr1")]
        wo_ctx.close()

        with ExitStack() as ctx:
            raw = [sb(ctx, f"raw{i}", [128, DW]) for i in range(3)]
            wh = [sb(ctx, f"eh{i}", [128, 3, GW], F32R) for i in range(2)]
            wl = [sb(ctx, f"el{i}", [128, 3, GW], F32R) for i in range(2)]
            gb = [sb(ctx, f"gb{i}", [128, 8]) for i in range(2)]
            xs = [sb(ctx, f"xs{i}", [128, 2, RW]) for i in range(2)]
            xh = [sb(ctx, f"xh{i}", [128, C, S], F32R) for i in range(2)]
            xl = [sb(ctx, f"xl{i}", [128, C, S], F32R) for i in range(2)]
            ga = [sb(ctx, f"ga{i}", [128, S]) for i in range(3)]
            up = [sb(ctx, f"up{i}", [128, S]) for i in range(3)]
            sg = [sb(ctx, f"sg{i}", [128, S]) for i in range(3)]
            ah = [sb(ctx, f"ah{i}", [128, C, S], F32R) for i in range(2)]
            al = [sb(ctx, f"al{i}", [128, C, S], F32R) for i in range(2)]
            ys = [sb(ctx, f"ys{i}", [128, D]) for i in range(2)]
            ww = [sb(ctx, f"ww{i}", [128, 2]) for i in range(3)]
            pw = sb(ctx, "pw", [128, 2, NE])
            gk = sb(ctx, "gk", [128, 4])
            gj = sb(ctx, "gj", [128, NE])
            gi = sb(ctx, "gi", [128, 1], U32)
            tab = sb(ctx, "tab", [2 * NT, 128])
            ids = sb(ctx, "ids", [128, 2 * NT])
            ti = sb(ctx, "ti", [128, 2 * NT], U32)
            cn = sb(ctx, "cn", [128, NE])
            ci = sb(ctx, "ci", [128, NE], I32)
            cj = sb(ctx, "cj", [128, NE], I32)
            nt = sb(ctx, "nt", [128, NE])
            en = sb(ctx, "en", [128, NE])
            sn = sb(ctx, "sn", [128, NE])
            b8 = sb(ctx, "b8", [128, NT, NE])
            Ei = sb(ctx, "Ei", [128, NT])
            ohE = sb(ctx, "ohE", [128, NT, NE])
            e0 = sb(ctx, "e0", [128, 1])
            pd = sb(ctx, "pd", [128, NT])
            gx = sb(ctx, "gx", [128, 2 * NT], U32)
            wx = sb(ctx, "wx", [128, NT], U32)
            ba = sb(ctx, "ba", [128, NT])

            def bc(ap, n):
                return ap.unsqueeze(2).to_broadcast([128, NT, n])

            def ch(fn, *w):
                last[0] = dve(fn, last[0], *w)
                return last[0]

            last = [run_t[0]]
            ch(lambda e: e.tensor_tensor(cn[:], run[:], EBASE, ALU.subtract), *over_b)
            ch(lambda e: e.tensor_scalar(ci[:], cn[:], 255.0, None, ALU.add))
            ch(lambda e: e.tensor_scalar(cj[:], ci[:], 8, None, ALU.logical_shift_right))
            ch(lambda e: e.tensor_copy(nt[:], cj[:]))
            ch(lambda e: e.tensor_tensor_scan(en[:], onef[:, 0:NE], nt[:], 0.0, ALU.mult, ALU.add), t_onef)
            ch(lambda e: e.tensor_tensor(sn[:], en[:], nt[:], ALU.subtract))
            ch(lambda e: e.tensor_tensor(b8[:], TI8, en[:].unsqueeze(1).to_broadcast([128, NT, NE]), ALU.is_ge))
            ch(lambda e: e.tensor_reduce(Ei[:], b8[:], AX, ALU.add))
            ch(lambda e: e.tensor_tensor(ohE[:], IT8, bc(Ei[:], NE), ALU.is_equal))
            ch(lambda e: e.tensor_scalar(gj[:], en[:], SPT, None, ALU.is_le))
            ch(lambda e: e.tensor_reduce(gk[:, 0:1], gj[:], AX, ALU.add))
            ch(lambda e: e.tensor_scalar(gj[:], IO8, gk[:, 0:1], None, ALU.is_equal))
            ch(lambda e: e.tensor_tensor(gj[:], gj[:], sn[:], ALU.mult))
            ch(lambda e: e.tensor_reduce(gk[:, 1:2], gj[:], AX, ALU.add))
            ch(lambda e: e.tensor_scalar(gk[:, 2:3], gk[:, 0:1], float(ER // 128), SPR, ALU.mult, ALU.add))
            ch(lambda e: e.scalar_tensor_tensor(out=gk[:, 3:4], in0=gk[:, 1:2], scalar=-2.0, in1=gk[:, 2:3],
                                                op0=ALU.mult, op1=ALU.add))
            ch(lambda e: e.tensor_scalar(gk[:, 2:3], gk[:, 3:4], float(TR), None, ALU.min))
            t_gi = ch(lambda e: e.tensor_copy(gi[:], gk[:, 2:3]))
            t_tab = dma("gpsimd", "tab", lambda e: e.indirect_dma_start(
                tab[:], None, slot.rearrange("(a n) o -> a (n o)", n=128),
                bass.IndirectOffsetOnAxis(ap=gi[0:2 * NT, :], axis=0)), t_gi, *over_b)
            ch(lambda e: e.tensor_scalar(e0[:], Ei[:, 0:1], -float(NE), None, ALU.add))
            ch(lambda e: e.tensor_scalar(pd[:], Ei[:], float(NE), e0[:, 0:1], ALU.is_equal, ALU.mult))
            ch(lambda e: e.tensor_tensor(Ei[:], Ei[:], pd[:], ALU.add))
            ch(lambda e: e.tensor_tensor(ohE[:], IT8, bc(Ei[:], NE), ALU.is_equal))
            ch(lambda e: e.tensor_scalar(ba[:], Ei[:], 128.0, PIDX, ALU.mult, ALU.add))
            t_wx = ch(lambda e: e.tensor_copy(wx[:], ba[:]))
            g_ids = pe(lambda e: nc.tensor.transpose(bank[0][:, 0:2 * NT], tab[:], ident[0:2 * NT, 0:2 * NT]), t_tab, *free[0])
            ch(lambda e: e.tensor_copy(ids[:], bank[0][:, 0:2 * NT]), g_ids)
            free[0] = [last[0]]
            t_ti = ch(lambda e: e.tensor_copy(ti[:], ids[:]))
            ch(lambda e: e.tensor_scalar(ids[:], ids[:], float(T - 1), None, ALU.min))
            t_gx = ch(lambda e: e.tensor_copy(gx[:], ids[:]))

            raw_free = [None] * 3
            wh_free = [[None] * 3, [None] * 3]
            gb_free = [None, None]
            xs_free = [[], []]
            xs_in = {}
            w_ok = {}
            rn = [0]

            def gather(key, dst, src, idx, *w):
                return dma("gpsimd", key, lambda e: e.indirect_dma_start(
                    dst, None, src, bass.IndirectOffsetOnAxis(ap=idx, axis=0)), *w)

            def fetch_x(i):
                for r in range(2):
                    z = gather(f"xs{i % 2}", xs[i % 2][:, r, :], hb, gx[:, 2 * i + r:2 * i + r + 1], t_gx, *xs_free[i % 2],
                               *(over_b if i < 2 else ()))
                xs_in[i] = z

            def fetch_w(i, part):
                src = (wga, wgb, wd)[part]
                n = DW if part == 1 else GW
                z = gather(f"raw{part}", raw[part][:, 0:n], src, wx[:, i:i + 1], t_wx, *(raw_free[part] or ()),
                           *(over_b if i == 0 else ()))
                w_in[(i, part)] = z

            w_in = {}

            def split_high(i, part):
                p = i % 2
                th = act(lambda e: e.activation(wh[p][:, part, :], raw[part][:, 0:GW], ACT.Copy), w_in[(i, part)],
                         wh_free[p][part])
                w_hi[(i, part)] = th

            def split_low(i, part):
                p = i % 2
                th = w_hi[(i, part)]
                if part == 1:
                    tb = dve(lambda e: e.tensor_copy(gb[p][:], raw[1][:, GW:DW]), w_in[(i, 1)], *(gb_free[p] or ()))
                tl = dve(lambda e: e.tensor_tensor(wl[p][:, part, :], raw[part][:, 0:GW], wh[p][:, part, :].bitcast(F32),
                                                   ALU.subtract), th)
                raw_free[part] = [th, tl]
                w_ok[(i, part)] = [th, tl] + ([tb] if part == 1 else [])
                if i + 1 < NT:
                    fetch_w(i + 1, part)

            w_hi = {}
            x_ok = {}
            xh_free = [None, None]
            ww_free = [None] * 3
            ww_t = {}

            def turn_x(i):
                p = i % 2
                for r in range(2):
                    k = 4 + r
                    g = pe(transposes(bank[k], xs[p][:, r, :], 4), xs_in[i], *free[k])
                    th, tl = split_psum(xh[p][:, :, r * 128:(r + 1) * 128], xl[p][:, :, r * 128:(r + 1) * 128],
                                        bank[k][:].rearrange("p (c n) -> p c n", c=4), g, xh_free[p])
                    free[k] = [th, tl]
                a_ = dve(lambda e: e.tensor_tensor(pw[:], xs[p][:, :, 512:520],
                                                   ohE[:, i, :].unsqueeze(1).to_broadcast([128, 2, NE]), ALU.mult), xs_in[i])
                ww_t[i] = dve(lambda e: e.tensor_reduce(ww[i % 3][:], pw[:], AX, ALU.add), a_, ww_free[i % 3])
                xs_free[p] = [g, a_]
                x_ok[i] = (th, tl)

            a_ok = {}
            a_free = [None, None]
            ga_free = [None] * 3
            up_free = [None] * 3
            sg_free = [None] * 3
            stage = {}

            def gate_up(i, m):
                p = i % 2
                n = C * i + m
                k = n % 4
                q = n % 3
                def emit(e):
                    for h in range(2):
                        o = bank[k][:, h * 256:(h + 1) * 256]
                        for c in range(C):
                            off = (c % 2) * 1024 + h * 512 + m * 128
                            lh = wh[p][:, c // 2, off:off + 128]
                            ll = wl[p][:, c // 2, off:off + 128]
                            nc.tensor.matmul(o, lh, xh[p][:, c, :], start=(c == 0), stop=False)
                            nc.tensor.matmul(o, lh, xl[p][:, c, :], start=False, stop=False)
                            last_ = nc.tensor.matmul(o, ll, xh[p][:, c, :], start=False, stop=(c == C - 1))
                    return last_
                g = pe(emit, *x_ok[i], *w_ok[(i, 0)], *w_ok[(i, 1)], *free[k])
                if m == C - 1:
                    xh_free[p] = g
                    wh_free[p][0] = wh_free[p][1] = g
                tb = w_ok[(i, 1)][2]
                g_ = dve(lambda e: e.tensor_scalar(ga[q][:], bank[k][:, 0:256], gb[p][:, m:m + 1], LIMIT, ALU.add, ALU.min),
                         g, tb, ga_free[q])
                u_ = act(lambda e: e.activation(up[q][:], bank[k][:, 256:512], ACT.Identity, bias=gb[p][:, 4 + m:5 + m]),
                         g_, up_free[q])
                s_ = act(lambda e: e.activation(sg[q][:], ga[q][:], ACT.Sigmoid, scale=ALPHA), g_, sg_free[q])
                free[k] = [u_, g_]
                gb_free[p] = (u_, g_)
                stage[n] = (g_, u_, s_)

            def activate(n):
                i, m = divmod(n, C)
                if not 0 <= i < NT:
                    return
                p = i % 2
                q = n % 3
                g_, u_, s_ = stage[n]
                v_ = dve(lambda e: e.tensor_scalar(up[q][:], up[q][:], LIMIT, -LIMIT, ALU.min, ALU.max), u_)
                y_ = dve(lambda e: e.scalar_tensor_tensor(out=up[q][:], in0=up[q][:], scalar=1.0, in1=ga[q][:],
                                                          op0=ALU.add, op1=ALU.mult), v_, g_)
                z_ = dve(lambda e: e.tensor_tensor(sg[q][:], up[q][:], sg[q][:], ALU.mult), y_, s_)
                h_ = act(lambda e: e.activation(ah[p][:, m, :], sg[q][:], ACT.Copy), z_, a_free[p])
                ga_free[q] = z_
                up_free[q] = z_
                stage[n] = h_

            def activate_low(n):
                i, m = divmod(n, C)
                if not 0 <= i < NT:
                    return
                p = i % 2
                q = n % 3
                h_ = stage[n]
                l_ = dve(lambda e: e.tensor_tensor(al[p][:, m, :], sg[q][:], ah[p][:, m, :].bitcast(F32), ALU.subtract), h_)
                sg_free[q] = l_
                a_ok[i] = (h_, l_)

            ys_free = [None, None]
            add_t = [None]

            def down(i, r):
                p = i % 2
                k = 6 + r
                lh = [ah[p][:, c, r * 128:(r + 1) * 128] for c in range(C)]
                ll = [al[p][:, c, r * 128:(r + 1) * 128] for c in range(C)]
                rh = [wh[p][:, 2, c * D:(c + 1) * D] for c in range(C)]
                rl = [wl[p][:, 2, c * D:(c + 1) * D] for c in range(C)]
                g = pe(mm3(bank[k][:], lh, ll, rh, rl), *a_ok[i], *w_ok[(i, 2)], *free[k])
                a_ = act(lambda e: e.activation(ys[r][:], bank[k][:], ACT.Copy, scale=ww[i % 3][:, r:r + 1]), g, ww_t[i], ys_free[r])
                free[k] = [a_]
                if r == 1:
                    wh_free[p][2] = g
                    a_free[p] = g
                    ww_free[i % 3] = a_
                return a_

            def add_rows(i, toks):
                p = i % 2
                prev = add_t[0]
                for r in range(2):
                    z = dma("gpsimd", f"add{p}", lambda e, r=r: e.indirect_dma_start(
                        out, bass.IndirectOffsetOnAxis(ap=ti[:, 2 * i + r:2 * i + r + 1], axis=0), ys[r][:], None,
                        bounds_check=T - 1, oob_is_err=False, compute_op=ALU.add), toks[r], t_ti, *(prev or base_out))
                for r in range(2):
                    ys_free[r] = z
                add_t[0] = [z]

            for part in range(3):
                fetch_w(0, part)
            fetch_x(0)
            fetch_x(1)
            for part in range(2):
                split_high(0, part)
                split_low(0, part)
            turn_x(0)
            for i in range(NT + 1):
                for m in range(C):
                    n = C * i + m
                    if i < NT:
                        if m == 0 or m == 1:
                            if i + 1 < NT:
                                split_high(i + 1, m)
                        elif m == 2:
                            split_high(i, 2)
                        if m == 3:
                            split_low(i, 2)
                        elif m > 0 and i + 1 < NT:
                            split_low(i + 1, m - 1)
                        gate_up(i, m)
                    activate(n - 1)
                    activate_low(n - 2)
                    if m == 0 and i + 1 < NT:
                        turn_x(i + 1)
                        if i + 2 < NT:
                            fetch_x(i + 2)
                    if m == 2 and i > 0:
                        add_rows(i - 1, [down(i - 1, 0), down(i - 1, 1)])
            queues["sync"].append((None, [add_t[0][0]] + base_out[-2:], None, 0))

        block = top.enter_context(nc.Block())

        def drive(name):
            def body(e):
                seen = {}
                for fn, waits, sem, n in queues[name]:
                    for s, v in waits:
                        if seen.get(id(s), 0) < v:
                            e.wait_ge(s, v)
                            seen[id(s)] = v
                    if fn is not None:
                        fn(e).then_inc(sem, n)
            return body

        block.tensor(drive("tensor"))
        block.vector(drive("vector"))
        block.scalar(drive("scalar"))
        block.gpsimd(drive("gpsimd"))
        block.sync(drive("sync"))


def constants():
    p = np.arange(128)
    cst = np.zeros((2, 128, 128), np.float32)
    cst[0] = np.eye(128)
    cst[1] = p[:, None] < p[None, :]
    cm = np.zeros((128, 520), np.float32)
    cm[:, 0:32] = np.tile(np.arange(8), 4)
    cm[:, 32:40] = np.arange(8) * ER
    cm[:, 56] = p
    cm[:, 57] = (p < 8) | (p >= 16)
    cm[:, 58] = (p >= 8) & (p < 16)
    cm[:, 60] = p // 2
    cm[:, 61] = p
    i = np.arange(NT)
    cm[:, 136:136 + 8 * NT] = np.repeat(i, 8)
    cm[:, 320:320 + 8 * NT] = np.tile(np.arange(8), NT)
    cm[:, 504:520] = p[:, None] + 128 * np.arange(16)[None, :]
    return cst, cm


def kernel(**inputs):
    import concourse.bacc as _bacc
    from concourse import mybir as _mybir
    from concourse.bass_utils import run_bass_kernel_spmd as _run

    g = {k: np.asarray(v) for k, v in inputs.items()}
    a = "L0_xattn_"
    f = "L0_ffn_"
    cst, cm = constants()
    cm[:, 40:56] = np.tile(g[f + "router_bias"], 2)[None, :]
    gu = g[f + "gate_up_proj"].reshape(NE, C, 128, C, 128, 2).transpose(0, 2, 1, 5, 3, 4).reshape(NE * 128, C, 1024)
    dn = g[f + "down_proj"].reshape(NE, C, 128, D).transpose(0, 2, 1, 3).reshape(NE * 128, C * D)
    gbias = g[f + "gate_up_proj_bias"].reshape(NE, C, 128, 2).transpose(0, 2, 3, 1).reshape(NE * 128, 8)
    arrays = {
        "in_x": g["x"].reshape(T, D),
        "in_ctxT": g["ctx_2048"].transpose(0, 2, 1).reshape(B, C, 128, S).transpose(0, 2, 1, 3).reshape(B, 128, C * S),
        "in_w": np.stack([g[a + n].T.reshape(C, 128, D).transpose(1, 0, 2).reshape(128, C * D)
                          for n in ("w_q", "w_k_img", "w_v_img", "w_o")]),
        "in_bias": np.stack([np.broadcast_to(g[a + n], (128, D))
                             for n in ("b_q", "b_k_img", "b_v_img", "g_q", "g_k_img", "b_o")]),
        "in_bd3": np.concatenate([g[f + "down_proj_bias"]] * 3),
        "in_rwT": g[f + "router_weight"].T.reshape(C, 128, NE).transpose(1, 0, 2).reshape(128, C * NE),
        "in_wga": gu[:, 0:2].reshape(NE * 128, GW),
        "in_wgb": np.concatenate([gu[:, 2:4].reshape(NE * 128, GW), gbias], axis=1),
        "in_wd": dn,
        "in_cst": cst,
        "in_cm": cm,
    }
    arrays = {k: np.ascontiguousarray(v) for k, v in arrays.items()}
    nc = _bacc.Bacc("TRN2", target_bir_lowering=False, num_devices=1)
    args = [nc.dram_tensor(k, v.shape, _mybir.dt.from_np(v.dtype), kind="ExternalInput").ap() for k, v in arrays.items()]
    args.append(nc.dram_tensor("out_0", (T, D), _mybir.dt.float32, kind="ExternalOutput").ap())
    program(nc, *args)
    r = _run(nc, [arrays], core_ids=[0])
    return r.results[0]["out_0"].reshape(B, S, D)
```

```python
from contextlib import ExitStack

import numpy as np

import concourse.bass as bass
from concourse import mybir

F32 = mybir.dt.float32
F32R = mybir.dt.float32r
BF16 = mybir.dt.bfloat16
U32 = mybir.dt.uint32
I32 = mybir.dt.int32
ALU = mybir.AluOpType
ACT = mybir.ActivationFunctionType
AX = mybir.AxisListType.X

B = 8
S = 256
D = 512
NH = 16
HD = 32
C = 4
NE = 8
T = 2048
LN_EPS = 1e-5
RMS_EPS = 1e-6
SCALE = 1.0 / float(np.sqrt(np.float32(HD)))
ALPHA = 1.702
LIMIT = 7.0
NT = 23
ER = 2048
RW = 520
SKIP = 4096
TR = NE * ER // 128
GW = 2048
DW = 2056


def program(nc, x, ctxT, wqkvo, bias, bd3, rwT, wga, wgb, wd, cst, cm, out):
    qs = [nc.dram_tensor(f"qs{b}", (2, HD, NH * S), F32, kind="Internal").ap() for b in range(B)]
    ks = [nc.dram_tensor(f"ks{b}", (2, HD, NH * S), F32, kind="Internal").ap() for b in range(B)]
    vs = [nc.dram_tensor(f"vs{b}", (128, 2 * D), F32, kind="Internal").ap() for b in range(B)]
    hb = nc.dram_tensor("hb", (T, RW), F32, kind="Internal").ap()
    slot = nc.dram_tensor("slot", ((TR + 1) * 128, 1), F32, kind="Internal").ap()

    with ExitStack() as top:
        queues = {n: [] for n in ("tensor", "vector", "scalar", "gpsimd", "sync")}
        done = {n: top.enter_context(nc.semaphore(f"done_{n}")) for n in ("tensor", "vector", "scalar", "gpsimd")}
        count = {n: 0 for n in done}
        dsem = {}
        dcount = {}

        def op(eng, fn, *waits):
            count[eng] += 1
            queues[eng].append((fn, [w for w in waits if w is not None], done[eng], 1))
            return (done[eng], count[eng])

        def pe(fn, *waits):
            return op("tensor", fn, *waits)

        def dve(fn, *waits):
            return op("vector", fn, *waits)

        def act(fn, *waits):
            return op("scalar", fn, *waits)

        def pool(fn, *waits):
            return op("gpsimd", fn, *waits)

        def dma(eng, key, fn, *waits):
            if key not in dsem:
                dsem[key] = top.enter_context(nc.semaphore(f"d_{key}"))
                dcount[key] = 0
            dcount[key] += 16
            queues[eng].append((fn, [w for w in waits if w is not None], dsem[key], 16))
            return (dsem[key], dcount[key])

        def load(key, dst, src, *waits, eng="sync"):
            return dma(eng, key, lambda e: e.dma_start(dst, src), *waits)

        def sb(ctx, name, shape, dt=F32, side=None):
            return ctx.enter_context(nc.sbuf_tensor(name, shape, dt, side=side))

        bank = [top.enter_context(nc.psum_tensor(f"bank{i}", [128, 512], F32)) for i in range(8)]
        free = [[] for _ in range(8)]

        ident = sb(top, "ident", [128, 128])
        cstt = sb(top, "cstt", [128, 256])
        tri = sb(top, "tri", [128, 128], BF16)
        ones = sb(top, "ones", [128, 128], BF16)
        onef = sb(top, "onef", [128, 32])
        cmt = sb(top, "cmt", [128, cm.shape[1]])
        half = sb(top, "half", [128, 2])
        run = sb(top, "run", [128, NE])
        rw = sb(top, "rw", [128, C * NE])
        t_ones = dve(lambda e: e.memset(ones[:], 1.0))
        t_onef = dve(lambda e: e.memset(onef[:], 1.0))
        t_half = dve(lambda e: e.memset(half[:], -0.5))
        IOTA = cmt[:, 0:32].rearrange("p (t j e) -> p t j e", t=2, j=2)
        IO8 = cmt[:, 0:8]
        EBASE = cmt[:, 32:40]
        RB = cmt[:, 40:56]
        PIDX = cmt[:, 56:57]
        MH = cmt[0:24, 57:58]
        ML = cmt[0:24, 58:59]
        TI8 = cmt[:, 136:136 + 8 * NT].rearrange("p (i e) -> p i e", e=8)
        IT8 = cmt[:, 320:320 + 8 * NT].rearrange("p (i e) -> p i e", e=8)
        TOK = cmt[:, 504:520]
        SPT = cmt[:, 60:61]
        SPR = cmt[:, 61:62]
        gk = sb(top, "gk", [128, 4])
        gj = sb(top, "gj", [128, NE])
        gi = sb(top, "gi", [128, 1], U32)
        tab = sb(top, "tab", [2 * NT, 128])
        ids = sb(top, "ids", [128, 2 * NT])
        ti = sb(top, "ti", [128, 2 * NT], U32)
        cn = sb(top, "cn", [128, NE])
        ci = sb(top, "ci", [128, NE], I32)
        cj = sb(top, "cj", [128, NE], I32)
        nt = sb(top, "nt", [128, NE])
        en = sb(top, "en", [128, NE])
        sn = sb(top, "sn", [128, NE])
        b8 = sb(top, "b8", [128, NT, NE])
        Ei = sb(top, "Ei", [128, NT])
        ohE = sb(top, "ohE", [128, NT, NE])
        e0 = sb(top, "e0", [128, 1])
        pd = sb(top, "pd", [128, NT])
        gx = sb(top, "gx", [128, 2 * NT], U32)
        wx = sb(top, "wx", [128, NT], U32)
        ba = sb(top, "ba", [128, NT])
        skips = sb(top, "skips", [128, TR + 1])
        t_skip = pool(lambda e: e.memset(skips[:], float(SKIP)))

        agenda = {}
        now = [0]

        def after(n, fn):
            agenda.setdefault(now[0] + n, []).append(fn)

        def step_on():
            now[0] += 1
            todo = agenda.setdefault(now[0], [])
            while todo:
                todo.pop(0)()
            del agenda[now[0]]

        def mm3(o, lh, ll, rh, rl):
            def emit(e):
                n = len(lh)
                last = None
                for c in range(n):
                    for j, (a, b) in enumerate(((lh[c], rh[c]), (lh[c], rl[c]), (ll[c], rh[c]))):
                        last = nc.tensor.matmul(o, a, b, start=(c == 0 and j == 0), stop=(c == n - 1 and j == 2))
                return last
            return emit

        def transposes(o, src, n, np_=128, w=128):
            def emit(e):
                for k in range(n):
                    last = nc.tensor.transpose(o[:, k * np_:(k + 1) * np_], src[:, k * w:(k + 1) * w],
                                               ident[0:np_, 0:np_])
                return last
            return emit

        def split_psum(hi, lo, src, ready, *waits):
            th = act(lambda e: e.activation(hi, src, ACT.Copy), ready, *waits)
            tl = dve(lambda e: e.tensor_tensor(lo, src, hi.bitcast(F32), ALU.subtract), th)
            return th, tl

        v_out = [None] * B
        q_out = [None] * B
        k_out = [None] * B
        wo_ctx = ExitStack()
        whi3 = sb(wo_ctx, "wohi", [128, C * D], F32R)
        wlo3 = sb(wo_ctx, "wolo", [128, C * D], F32R)
        qst = [sb(wo_ctx, "qst0", [128, NH, S], F32R)]
        bo = sb(wo_ctx, "bo", [128, D])
        bdh = sb(wo_ctx, "bdh", [24, D], F32R)
        bds = sb(wo_ctx, "bds", [24, D], F32R)
        early = ExitStack()
        wraw = [sb(early, f"wraw{i}", [128, C * D], side="right") for i in range(2)]
        bdr = sb(early, "bdr", [24, D], side="right")
        bdl = sb(early, "bdl", [24, D], side="right")
        mx = [sb(wo_ctx, f"mx{i}", [128, 2, NH]) for i in range(2)]
        st_in = {}
        st_free = [None] * 3
        v_in = {}
        vb = []
        v_free = []
        def load_values(b):
            v_in[b] = load(f"vb{b % 3}", vb[b % 3][:], vs[b], v_out[b], *st_free[b % 3], *v_free)

        def load_stacks(b, pace):
            i = b % 3
            w = list(st_free[i])

            def part(dst, src, tok, quad, plane):
                st_in[b] = load(f"st{i}", dst[i][32 * quad:32 * quad + 32, :, :].bitcast(F32)
                                .rearrange("p h n -> p (h n)"), src[b][plane], tok[b], *w)

            parts = [lambda q=q, p=p: part(qst, qs, q_out, q, p) for q, p in enumerate((0, 0, 1))] + \
                    [lambda q=q, p=p: part(kst, ks, k_out, q, p) for q, p in enumerate((0, 1, 0))]
            if b > 1:
                parts.append(lambda: load_values(b))
            for n, fn in enumerate(parts):
                if pace:
                    after(pace * n + 1, fn)
                else:
                    fn()

        mx_t = {}
        mx_free = [[], []]

        def head(b, cb, h4):
            return h4 * 4 + cb

        def score_max(b, n, k=None):
            cb, h4 = divmod(n, 4)
            s_ = head(b, cb, h4)
            i = b % 3
            if k is None:
                k = (0, 1, 5)[(NH * b + n) % 3]
            def emit(e):
                for t in range(2):
                    last = nc.tensor.matmul(bank[k][:, t * 256:(t + 1) * 256],
                                            qst[i][0:96, s_, t * 128:(t + 1) * 128], kst[i][0:96, s_, :],
                                            start=True, stop=True)
                return last
            g = pe(emit, st_in[b], *free[k])

            def reduce():
                d_ = dve(lambda e: e.tensor_reduce(mx[b % 2][:, :, n], bank[k][:].rearrange("p (t n) -> p t n", t=2),
                                                   AX, ALU.max), g, *mx_free[b % 2])
                free[k] = [d_]
                mx_t[(b, n // 8)] = d_
            free[k] = None
            after(1, reduce)


        with ExitStack() as ctx:
            WH = [sb(ctx, f"wh{i}", [128, C * D], F32R) for i in range(3)] + [whi3]
            WL = [sb(ctx, f"wl{i}", [128, C * D], F32R) for i in range(3)] + [wlo3]
            bi = [sb(ctx, f"bi{i}", [128, D]) for i in range(5)]
            xt = [sb(ctx, f"xt{i}", [128, 2, D]) for i in range(2)]
            st6 = sb(ctx, "st6", [128, 2, 6])
            mv = sb(ctx, "mv", [128, 2, 2])
            ve = sb(ctx, "ve", [128, 2])
            rs = sb(ctx, "rs", [128, 2])
            hn = [sb(ctx, f"hn{i}", [128, D]) for i in range(2)]
            hth = [qst[0][:, 0:4, :], sb(ctx, "hth1", [128, C, S], F32R)]
            htl = [qst[0][:, 4:8, :], sb(ctx, "htl1", [128, C, S], F32R)]
            cr = [sb(ctx, f"cr{i}", [128, C * S]) for i in range(2)]
            cth = [qst[0][:, 8:12, :].rearrange("p c n -> p (c n)"), sb(ctx, "cth1", [128, C * S], F32R)]
            ctl = [qst[0][:, 12:16, :].rearrange("p c n -> p (c n)"), sb(ctx, "ctl1", [128, C * S], F32R)]
            pf = [sb(ctx, f"pf{i}", [128, D]) for i in range(4)]
            sqj = sb(ctx, "sqj", [128, D])
            ss = [sb(ctx, f"ss{i}", [128, 1]) for i in range(4)]
            sr = [sb(ctx, f"sr{i}", [128, 1]) for i in range(4)]
            qth = [sb(ctx, f"qth{i}", [128, C, S], F32R) for i in range(2)]
            qtl = [sb(ctx, f"qtl{i}", [128, C, S], F32R) for i in range(2)]
            vt = [sb(ctx, f"vt{i}", [128, 2 * D]) for i in range(2)]

            x_in = {}
            x_free = [None, None]
            c_in = {}
            c_free = [[], []]
            ht_free = [None, None]
            ct_free = [None, None]
            hn_free = [None, None]

            def load_batch(b):
                p = b % 2
                x_in[b] = load(f"x{p}", xt[p][:], x[b * S:(b + 1) * S, :].rearrange("(t p) d -> p t d", p=128), x_free[p])
                c_in[b] = load(f"c{p}", cr[p][:], ctxT[b], *c_free[p])

            b_in = None
            w_t = {}
            ht_t = {}
            ct_t = {}
            ring = {"m": 0, "t": 0}

            def mbank():
                ring["m"] += 1
                return (ring["m"] - 1) % 4

            def tbank():
                ring["t"] += 1
                return 4 + (ring["t"] - 1) % 4

            def layer_norm(b):
                p = b % 2
                for t in range(2):
                    s_ = dve(lambda e, t=t: e.bn_stats(st6[:, t, :], xt[p][:, t, :]), x_in[b], ln_free[0])
                for t in range(2):
                    a_ = dve(lambda e, t=t: e.bn_aggr(mv[:, t, :], st6[:, t, :]), s_)
                v_ = dve(lambda e: e.tensor_scalar(ve[:], mv[:, :, 1], LN_EPS, None, ALU.add), a_)
                ln_r[0] = pool(lambda e: e.tensor_tensor(rs[:], ve[:], half[:], ALU.pow), v_, t_half)

            def ln_scale(b):
                p = b % 2
                for t in range(2):
                    n_ = dve(lambda e, t=t: e.tensor_scalar(hn[t][:], xt[p][:, t, :], mv[:, t, 0:1], rs[:, t:t + 1],
                                                            ALU.subtract, ALU.mult), ln_r[0], hn_free[t])
                    ln_t[(b, t)] = n_
                ln_free[0] = n_
                x_free[p] = n_

            ln_r = [None]
            ln_free = [None]
            ln_t = {}

            def ln_transposes(b):
                p = b % 2
                turned = []
                for t in range(2):
                    k = tbank()
                    g = pe(transposes(bank[k], hn[t], 4), ln_t[(b, t)], t_id, *free[k])
                    hn_free[t] = g
                    turned.append((k, g))

                def evacuate():
                    for t, (k, g) in enumerate(turned):
                        src = bank[k][:].rearrange("p (c n) -> p c n", c=4)
                        th, tl = split_psum(hth[p][:, :, t * 128:(t + 1) * 128], htl[p][:, :, t * 128:(t + 1) * 128],
                                            src, g, ht_free[p])
                        free[k] = [th, tl]
                    ht_t[b] = (th, tl)
                for k, g in turned:
                    free[k] = None
                return evacuate

            def ctx_split(b):
                p = b % 2
                th = act(lambda e: e.activation(cth[p][:], cr[p][:], ACT.Copy), c_in[b], ct_free[p])
                tl = dve(lambda e: e.tensor_tensor(ctl[p][:], cr[p][:], cth[p][:].bitcast(F32), ALU.subtract), th)
                ct_t[b] = (th, tl)
                c_free[p] = [th, tl]

            def load_w(i, p, *waits):
                return load(f"w{p}", wraw[p][:], wqkvo[i], *waits)

            def split_w(i, p, ready):
                th = act(lambda e: e.activation(WH[i][:], wraw[p][:], ACT.Copy), ready)
                tl = dve(lambda e: e.tensor_tensor(WL[i][:], wraw[p][:], WH[i][:].bitcast(F32), ALU.subtract), th)
                w_t[i] = (th, tl)
                return tl

            x_in[0] = load("x0", xt[0][:], x[0:S, :].rearrange("(t p) d -> p t d", p=128))
            w0 = load_w(0, 0)
            t_id = load("cst", ident[:], cst[0])
            c_in[0] = load("c0", cr[0][:], ctxT[0])
            w1 = load_w(1, 1)
            for i, dst in enumerate(bi):
                b_in = load("bi", dst[:], bias[i])
            layer_norm(0)
            ln_scale(0)
            evacuate_0 = ln_transposes(0)
            r0 = split_w(0, 0, w0)
            evacuate_0()
            w2 = load_w(2, 0, r0)
            r1 = split_w(1, 1, w1)
            load_batch(1)
            w3 = load_w(3, 1, r1)
            ctx_split(0)
            b_in_o = load("bo", bo[:], bias[5])
            t_bd = load("bd", bdr[:], bd3)
            t_cm = load("cm", cmt[:], cm)
            t_tr = load("tri", cstt[:, 0:128], cst[1])
            t_rw = load("rw", rw[:], rwT)
            t_slot = load("slot", slot.rearrange("(p n) o -> p (n o)", p=128), skips[:], t_skip)

            def bd_split():
                th = act(lambda e: e.activation(bdh[:], bdr[:], ACT.Copy), t_bd)
                tl = dve(lambda e: e.tensor_tensor(bdl[:], bdr[:], bdh[:].bitcast(F32), ALU.subtract), th)
                tm = dve(lambda e: e.tensor_scalar(bdl[:], bdl[:], ML, None, ALU.mult), tl, t_cm)
                return dve(lambda e: e.scalar_tensor_tensor(out=bds[:], in0=bdh[:].bitcast(F32), scalar=MH, in1=bdl[:],
                                                            op0=ALU.mult, op1=ALU.add), tm)

            pf_free = [None] * 4
            qt_free = [None, None]
            vt_free = [None, None]
            units = 0

            def project(b, kind, t):
                nonlocal units
                p = b % 2
                k = mbank()
                if kind == 0:
                    lh = [hth[p][:, c, t * 128:(t + 1) * 128] for c in range(C)]
                    ll = [htl[p][:, c, t * 128:(t + 1) * 128] for c in range(C)]
                    ready = ht_t[b]
                else:
                    lh = [cth[p][:, c * S + t * 128:c * S + (t + 1) * 128] for c in range(C)]
                    ll = [ctl[p][:, c * S + t * 128:c * S + (t + 1) * 128] for c in range(C)]
                    ready = ct_t[b]
                rh = [WH[kind][:, c * D:(c + 1) * D] for c in range(C)]
                rl = [WL[kind][:, c * D:(c + 1) * D] for c in range(C)]
                g = pe(mm3(bank[k][:], lh, ll, rh, rl), *ready, *w_t[kind], *free[k])
                if t == 1 and kind == 0:
                    ht_free[p] = g
                if t == 1 and kind == 2:
                    ct_free[p] = g
                if kind == 2:
                    def bias_v():
                        a = dve(lambda e: e.tensor_tensor(vt[p][:, t * D:(t + 1) * D], bank[k][:], bi[2][:], ALU.add),
                                g, b_in, vt_free[p])
                        free[k] = [a]
                        if t == 1:
                            vt_free[p] = v_out[b] = load(f"v{p}", vs[b], vt[p][:], a)
                    after(1, bias_v)
                    return
                u = units % 4
                units += 1

                def bias():
                    a = dve(lambda e: e.tensor_tensor(pf[u][:], bank[k][:], bi[kind][:], ALU.add), g, b_in, pf_free[u])
                    free[k] = [a]
                    s_ = act(lambda e: e.activation(sqj[:], pf[u][:], ACT.Square, accum_out=ss[u][:]), a)

                    def root():
                        m_ = dve(lambda e: e.tensor_scalar(ss[u][:], ss[u][:], 1.0 / D, RMS_EPS, ALU.mult, ALU.add), s_)
                        r_ = pool(lambda e: e.tensor_tensor(sr[u][:], ss[u][:], half[:, 0:1], ALU.pow), m_, t_half)
                        after(1, lambda: normalise(b, kind, t, u, r_))
                    after(1, root)
                after(1, bias)

            def normalise(b, kind, t, u, r_):
                n_ = dve(lambda e: e.scalar_tensor_tensor(out=pf[u][:], in0=pf[u][:], scalar=sr[u][:, 0:1],
                                                          in1=bi[3 + kind][:], op0=ALU.mult, op1=ALU.mult), r_)
                after(1, lambda: to_heads(b, kind, t, u, n_))

            def to_heads(b, kind, t, u, n_):
                k = tbank()
                g = pe(transposes(bank[k], pf[u], 4), n_, *free[k])
                pf_free[u] = g
                src = bank[k][:].rearrange("p (c n) -> p c n", c=4)

                def evacuate():
                    th, tl = split_psum(qth[kind][:, :, t * 128:(t + 1) * 128], qtl[kind][:, :, t * 128:(t + 1) * 128],
                                        src, g, qt_free[kind])
                    free[k] = [th, tl]
                    if t == 1:
                        store_heads(b, kind, th, tl)
                after(1, evacuate)

            def store_heads(b, kind, th, tl):
                dst = (qs if kind == 0 else ks)[b]
                for n, (tile, tok) in enumerate(((qth[kind], th), (qtl[kind], tl))):
                    for h4 in range(4):
                        o = dst[n].rearrange("d (h m) -> d h m", h=4)[:, h4, :]
                        i = tile[32 * h4:32 * h4 + 32, :, :].bitcast(F32).rearrange("p c n -> p (c n)")
                        z = load(f"s{kind}", o, i, tok)
                qt_free[kind] = z
                (q_out if kind == 0 else k_out)[b] = z

            for b in range(B):
                order = ((0, 0), (1, 0), (2, 0), (0, 1), (1, 1), (2, 1)) if b else \
                    ((0, 0), (0, 1), (1, 0), (1, 1), (2, 0), (2, 1))
                for n, (kind, t) in enumerate(order):
                    step_on()
                    if b == 0 and n == 2:
                        split_w(2, 0, w2)
                    if b == B - 1 and n == 0:
                        st_free[0] = [ht_free[0], ct_free[0], *w_t[2], *w_t[3], t_bds]
                        load_stacks(0, 0)
                    project(b, kind, t)
                    if b == B - 1 and n >= 3:
                        score_max(0, n - 3, tbank())
                    if n == 0 and b + 2 < B:
                        load_batch(b + 2)
                    if b + 1 < B:
                        if n == 1:
                            layer_norm(b + 1)
                        elif n == 2:
                            ln_scale(b + 1)
                            ctx_split(b + 1)
                        elif n == 3:
                            after(1, ln_transposes(b + 1))
                    if b == 1 and n == 3:
                        split_w(3, 1, w3)
                    if b == 2 and n == 3:
                        t_tri = dve(lambda e: e.tensor_copy(tri[:], cstt[:, 0:128]), t_tr)
                        t_run = dve(lambda e: e.tensor_copy(run[:], EBASE), t_cm)
                        t_bds = bd_split()
                        early.close()
                        kst = [sb(wo_ctx, "kst0", [128, NH, S], F32R, side="right")]
            projected = (done["tensor"], count["tensor"])

        with ExitStack() as ctx:
            for i in (1, 2):
                qst.append(sb(ctx, f"qst{i}", [128, NH, S], F32R))
                kst.append(sb(ctx, f"kst{i}", [128, NH, S], F32R))
            vb += [sb(ctx, f"vb{i}", [128, 2 * D]) for i in range(3)]
            nm = [sb(ctx, f"nm{i}", [8, 2, 128]) for i in range(2)]
            pt = [sb(ctx, f"pt{i}", [128, 512]) for i in range(6)]
            rec = [sb(ctx, f"rec{i}", [128, S]) for i in range(1)]
            of = [sb(ctx, f"of{i}", [128, S]) for i in range(2)]
            oh_ = [sb(ctx, f"oh{i}", [128, C, S], F32R) for i in range(2)]
            ol_ = [sb(ctx, f"ol{i}", [128, C, S], F32R) for i in range(2)]
            xb = [sb(ctx, f"xb{i}", [128, D]) for i in range(4)]
            hr = [sb(ctx, f"hr{i}", [128, RW]) for i in range(2)]
            h2t = [sb(ctx, f"h2t{i}", [128, 512]) for i in range(2)]
            st6B = sb(ctx, "st6b", [128, 6])
            mvB = [sb(ctx, f"mvb{i}", [128, 2]) for i in range(2)]
            veB = [sb(ctx, f"veb{i}", [128, 1]) for i in range(2)]
            rsB = [sb(ctx, f"rsb{i}", [128, 1]) for i in range(2)]
            nmB = [sb(ctx, f"nmb{i}", [128, 1]) for i in range(2)]
            nm_free = [None, None]
            lg = sb(ctx, "lg", [128, 2, NE])
            m8 = sb(ctx, "m8", [128, 2, 8])
            ix = sb(ctx, "ix", [128, 2, 8], U32)
            ixf = sb(ctx, "ixf", [128, 2, 8])
            oht = sb(ctx, "oht", [128, 2, 2, NE])
            dd = sb(ctx, "dd", [128, 2])
            ee = sb(ctx, "ee", [128, 2])
            se = sb(ctx, "se", [128, 2])
            wa = sb(ctx, "wa", [128, 2])
            wb = sb(ctx, "wb", [128, 2])
            tmp8 = sb(ctx, "tmp8", [128, 2, NE])
            M = sb(ctx, "M", [128, 2, NE], BF16)
            pos = sb(ctx, "pos", [128, 2, NE])
            pr = sb(ctx, "pr", [128, 2, 2, NE])
            sl = sb(ctx, "sl", [128, 4])
            si = [sb(ctx, f"si{i}", [128, 4], U32) for i in range(2)]
            sc3 = sb(ctx, "sc3", [128, 2, 3, NE])
            s3t = sb(ctx, "s3t", [24, 256], F32R)
            ob = [sb(ctx, f"ob{i}", [128, D]) for i in range(2)]

            st_free[1] = [projected]
            load_stacks(1, 0)
            for n in range(6):
                step_on()
                score_max(0, n + 3, tbank())
            step_on()
            over_a = [(done[n], count[n]) for n in ("tensor", "vector", "scalar", "gpsimd")]
            stored_a = [(dsem[k], dcount[k]) for k in ("s0", "s1", "v0", "v1")]
            m_in = {}
            v_free += over_a
            st_free[2] = over_a
            one_t = []
            for i, w in enumerate((st_free[0], st_free[1], over_a)):
                one_t.append(pool(lambda e, i=i: e.memset(kst[i][96:97, :, :].bitcast(F32), 1.0), *w,
                                  (done["gpsimd"], count["gpsimd"])))

            def send_max(b, half_):
                k = 6
                def emit(e):
                    for t in range(2):
                        last = nc.tensor.transpose(bank[k][0:8, t * 128:(t + 1) * 128],
                                                   mx[b % 2][:, t, 8 * half_:8 * half_ + 8], ident[:])
                    return last
                g = pe(emit, mx_t[(b, half_)], *free[k])
                if half_:
                    mx_free[b % 2] = [g]
                a_ = act(lambda e: e.activation(nm[half_][:].rearrange("h t n -> h (t n)"), bank[k][0:8, 0:256],
                                                ACT.Copy, scale=-1.0), g, m_in.get((b - 1, half_)), *(over_a if b == 0 else ()))
                free[k] = [a_]
                row = qst[b % 3][96:97, :, :].bitcast(F32).rearrange("p (h c) n -> p c h n", c=4)
                for j in range(2):
                    m_in[(b, half_)] = load(f"m{half_}", row[:, 2 * half_ + j, :, :],
                                            nm[half_][4 * j:4 * j + 4, :, :].rearrange("h t n -> h (t n)"), a_,
                                            eng="scalar" if b == 0 and half_ == 0 else "sync")

            pt_free = [None] * 6
            pt_t = {}
            pn = [0]

            def probs(b, n):
                cb, h4 = divmod(n, 4)
                s_ = head(b, cb, h4)
                i = b % 3
                k = 2 + n % 2
                u = pn[0] % 6
                pn[0] += 1
                def emit(e):
                    for t in range(2):
                        last = nc.tensor.matmul(bank[k][:, t * 256:(t + 1) * 256],
                                                kst[i][0:97, s_, t * 128:(t + 1) * 128], qst[i][0:97, s_, :],
                                                start=True, stop=True)
                    return last
                g = pe(emit, st_in[b], m_in[(b, n // 8)], one_t[b % 3], *free[k])
                a_ = act(lambda e: e.activation(pt[u][:], bank[k][:], ACT.Exp, scale=SCALE), g, pt_free[u])
                free[k] = [a_]
                pt_t[(b, n)] = (u, a_)
                return g

            o_t = {}
            of_free = [None, None]
            o_free = [None, None]
            gn = [0]

            def values(b, g4):
                k = 4
                f = gn[0] % 2
                gn[0] += 1
                us = [pt_t[(b, 4 * g4 + j)] for j in range(4)]
                def emit(e):
                    for half_ in range(2):
                        for t in range(2):
                            for j in range(4):
                                lhs = onef[:] if half_ else vb[b % 3][:, t * D + g4 * 128 + 32 * j:t * D + g4 * 128 + 32 * j + 32]
                                last = nc.tensor.matmul(bank[k][32 * j:32 * j + 32, half_ * 256:half_ * 256 + 256], lhs,
                                                        pt[us[j][0]][:, t * 256:(t + 1) * 256],
                                                        start=(t == 0), stop=(t == 1))
                    return last
                g = pe(emit, *[u[1] for u in us], v_in[b], t_onef, *free[k])
                for u in us:
                    pt_free[u[0]] = g

                free[k] = None
                rs_ = []

                def invert(a):
                    rs_.append(dve(lambda e: e.reciprocal(rec[0][:, a:a + 128], bank[k][:, 256 + a:384 + a]), g))

                def divide():
                    m_ = dve(lambda e: e.tensor_tensor(of[f][:], bank[k][:, 0:256], rec[0][:], ALU.mult), rs_[1], of_free[f])
                    free[k] = [m_]
                    h_ = act(lambda e: e.activation(oh_[b % 2][:, g4, :], of[f][:], ACT.Copy), m_, o_free[b % 2],
                             *(stored_a if b < 2 else ()))
                    sub = dve if b == B - 1 and g4 >= 2 else pool
                    l_ = sub(lambda e: e.tensor_tensor(ol_[b % 2][:, g4, :], of[f][:], oh_[b % 2][:, g4, :].bitcast(F32),
                                                       ALU.subtract), h_, o_free[b % 2])
                    of_free[f] = l_
                    o_t[b] = (*o_t.get(b, ()), h_, l_)
                after(1, lambda: invert(0))
                after(2, lambda: invert(128))
                after(3, divide)
                return g

            xb_free = [None] * 4
            xb_in = {}
            hr_free = [None, None]
            h2_t = {}
            ob_free = [None, None]
            base_out = []
            lg_t = {}

            def load_x(b):
                for t in range(2):
                    u = 2 * (b % 2) + t
                    z = load(f"xb{u}", xb[u][:], x[b * S + t * 128:b * S + (t + 1) * 128, :], xb_free[u],
                             *(over_a + stored_a if b < 2 else ()))

                    def add_bo(t=t, u=u, z=z):
                        xb_in[(b, t)] = pool(lambda e: e.tensor_tensor(xb[u][:], xb[u][:], bo[:], ALU.add), z, b_in_o, one_t[2])
                    if b < 2:
                        add_bo()
                    else:
                        after(6, add_bo)

            def out_project(b, t):
                k = 6 + t
                lh = [oh_[b % 2][:, c, t * 128:(t + 1) * 128] for c in range(C)]
                ll = [ol_[b % 2][:, c, t * 128:(t + 1) * 128] for c in range(C)]
                rh = [whi3[:, c * D:(c + 1) * D] for c in range(C)]
                rl = [wlo3[:, c * D:(c + 1) * D] for c in range(C)]
                g = pe(mm3(bank[k][:], lh, ll, rh, rl), *o_t[b], *w_t[3], *free[k])
                if t == 1:
                    o_free[b % 2] = g
                projected_o[0] = g
                free[k] = None

                u = 2 * (b % 2) + t

                def residual():
                    a_ = dve(lambda e: e.tensor_tensor(xb[u][:], bank[k][:], xb[u][:], ALU.add), g, xb_in[(b, t)])
                    free[k] = [a_]
                    s_ = dve(lambda e: e.bn_stats(st6B[:], xb[u][:]), a_)
                    s_ = dve(lambda e: e.bn_aggr(mvB[t][:], st6B[:]), s_, nm_free[t])
                    v_ = dve(lambda e: e.tensor_scalar(veB[t][:], mvB[t][:, 1:2], LN_EPS, None, ALU.add), s_)
                    r_ = pool(lambda e: e.tensor_tensor(rsB[t][:], veB[t][:], half[:, 0:1], ALU.pow), v_, nm_free[t])

                    def scale():
                        n_ = dve(lambda e: e.tensor_scalar(nmB[t][:], mvB[t][:, 0:1], rsB[t][:, 0:1], -1.0,
                                                           ALU.mult, ALU.mult), r_, nm_free[t])
                        h_ = act(lambda e: e.activation(hr[t][:, 0:512], xb[u][:], ACT.Identity, scale=rsB[t][:, 0:1],
                                                        bias=nmB[t][:, 0:1]), n_, hr_free[t])
                        nm_free[t] = h_
                        h2_t[(b, t)] = h_
                    after(1, scale)
                after(1, residual)

            projected_o = [None]
            h2t_free = [None, None]

            def router_turn(b, t):
                k = 7
                g = pe(transposes(bank[k], hr[t], 4), h2_t[(b, t)], *free[k])
                a_ = act(lambda e: e.activation(h2t[t][:], bank[k][:], ACT.Copy), g, h2t_free[t])
                free[k] = [a_]
                h2t_t[t] = a_

            h2t_t = [None, None]

            def router(b, t):
                k = 6
                def emit(e):
                    for c in range(C):
                        last = nc.tensor.matmul(bank[k][:, t * 8:t * 8 + 8], h2t[t][:, c * 128:(c + 1) * 128],
                                                rw[:, c * NE:(c + 1) * NE], start=(c == 0), stop=(c == C - 1))
                    return last
                g = pe(emit, h2t_t[t], t_rw, *free[k])
                h2t_free[t] = g
                free[k] = [g]
                lg_t[(b, t)] = g

            rk = [None]
            si_free = [None, None]

            def choose(b):
                k2 = 6
                c_ = dve(lambda e: e.tensor_tensor(lg[:].rearrange("p t e -> p (t e)"), bank[k2][:, 0:16], RB, ALU.add),
                         lg_t[(b, 0)], lg_t[(b, 1)])
                free[k2] = [c_]
                for t in range(2):
                    m_ = dve(lambda e, t=t: e.max(m8[:, t, :], lg[:, t, :]), c_)
                d_ = dve(lambda e: e.tensor_tensor(dd[:], m8[:, :, 1], m8[:, :, 0], ALU.subtract), m_)
                e_ = act(lambda e: e.activation(ee[:], dd[:], ACT.Exp), d_)
                for t in range(2):
                    i_ = dve(lambda e, t=t: e.max_index(ix[:, t, :], m8[:, t, :], lg[:, t, :]), m_)
                f_ = dve(lambda e: e.tensor_copy(ixf[:], ix[:]), i_)
                o_ = dve(lambda e: e.tensor_tensor(oht[:], IOTA, ixf[:, :, 0:2].unsqueeze(3).to_broadcast([128, 2, 2, NE]),
                                                   ALU.is_equal), f_)
                M_ = dve(lambda e: e.tensor_tensor(M[:], oht[:, :, 0, :], oht[:, :, 1, :], ALU.add), o_, rk[0])
                return M_, e_, o_

            def weigh(b, e_, o_):
                s_ = dve(lambda e: e.tensor_scalar(se[:], ee[:], 1.0, None, ALU.add), e_)
                w_ = dve(lambda e: e.reciprocal(wa[:], se[:]), s_)
                w2_ = dve(lambda e: e.tensor_tensor(wb[:], ee[:], wa[:], ALU.mult), w_)
                for t in range(2):
                    a_ = dve(lambda e, t=t: e.tensor_scalar(tmp8[:, t, :], oht[:, t, 0, :], wa[:, t:t + 1], None, ALU.mult), w_)
                for t in range(2):
                    y_ = dve(lambda e, t=t: e.scalar_tensor_tensor(out=hr[t][:, 512:520], in0=oht[:, t, 1, :],
                                                                   scalar=wb[:, t:t + 1], in1=tmp8[:, t, :],
                                                                   op0=ALU.mult, op1=ALU.add), a_, w2_, *([hr_free[t]]))
                for t in range(2):
                    z_ = dve(lambda e, t=t: e.tensor_copy(sc3[:, t, 0, :].bitcast(F32R), hr[t][:, 512:520]), y_, s3_free[0])
                for t in range(2):
                    dve(lambda e, t=t: e.tensor_copy(sc3[:, t, 1, :], sc3[:, t, 0, :]), z_)
                    z2 = dve(lambda e, t=t: e.tensor_tensor(sc3[:, t, 2, :], hr[t][:, 512:520], sc3[:, t, 0, :], ALU.subtract), z_)
                return y_, z2

            s3_free = [None]
            s3t_free = [None]

            def rank(b, M_):
                k = 7
                def emit(e):
                    r = bank[k]
                    nc.tensor.matmul(r[:, 0:8], tri[:], M[:, 0, :], start=True, stop=True)
                    nc.tensor.matmul(r[:, 8:16], tri[:], M[:, 1, :], start=True, stop=False)
                    nc.tensor.matmul(r[:, 8:16], ones[:], M[:, 0, :], start=False, stop=True)
                    nc.tensor.matmul(r[:, 16:24], ones[:], M[:, 0, :], start=True, stop=False)
                    return nc.tensor.matmul(r[:, 16:24], ones[:], M[:, 1, :], start=False, stop=True)
                g = pe(emit, M_, t_tri, t_ones, *free[k])
                rk[0] = g
                free[k] = None
                return g

            def place(b, g, y_):
                k = 7
                p_ = dve(lambda e: e.tensor_tensor(pos[:], bank[k][:, 0:16].rearrange("p (t e) -> p t e", t=2),
                                                   run[:].unsqueeze(1).to_broadcast([128, 2, NE]), ALU.add), g, t_run, run_t[0])
                n_ = dve(lambda e: e.tensor_tensor(run[:], bank[k][:, 16:24], run[:], ALU.add), p_)
                run_t[0] = n_
                free[k] = [n_]
                q_ = dve(lambda e: e.tensor_tensor(pr[:], oht[:], pos[:].unsqueeze(2).to_broadcast([128, 2, 2, NE]), ALU.mult), p_)
                r_ = dve(lambda e: e.tensor_reduce(sl[:], pr[:].rearrange("p t j e -> p (t j) e"), AX, ALU.add), q_)
                i_ = dve(lambda e: e.tensor_copy(si[b % 2][:], sl[:]), r_, si_free[b % 2])
                for t in range(2):
                    for j in range(2):
                        n = 2 * t + j
                        z = dma("gpsimd", f"sc{b % 2}", lambda e, n=n, t=t: e.indirect_dma_start(
                            slot, bass.IndirectOffsetOnAxis(ap=si[b % 2][:, n:n + 1], axis=0),
                            TOK[:, 2 * b + t:2 * b + t + 1], None), i_, t_slot)
                    hr_free[t] = load(f"hr{t}", hb[b * S + t * 128:b * S + (t + 1) * 128, :], hr[t][:], y_)
                si_free[b % 2] = z

            run_t = [None]

            def turn_scores(b, z2):
                k = 6
                def emit(e):
                    for t in range(2):
                        last = nc.tensor.transpose(bank[k][0:24, t * 128:(t + 1) * 128],
                                                   sc3[:, t, :, :].rearrange("p a e -> p (a e)"), ident[:])
                    return last
                g = pe(emit, z2, *free[k])
                s3_free[0] = g
                a_ = act(lambda e: e.activation(s3t[:], bank[k][0:24, 0:256], ACT.Copy), g, s3t_free[0])
                free[k] = [a_]
                return a_

            def add_bias(b, a_):
                gs = []
                for t in range(2):
                    k = 7 - t
                    g = pe(lambda e, t=t, k=k: nc.tensor.matmul(bank[k][:], s3t[:, t * 128:(t + 1) * 128], bds[:],
                                                                start=True, stop=True), a_, t_bds, *free[k])
                    free[k] = None
                    gs.append(g)
                s3t_free[0] = g

                def store():
                    for t in range(2):
                        k = 7 - t
                        d_ = dve(lambda e, t=t, k=k: e.tensor_tensor(ob[t][:], bank[k][:], xb[2 * (b % 2) + t][:], ALU.add), gs[t], ob_free[t])
                        free[k] = [d_]
                        xb_free[2 * (b % 2) + t] = d_
                        ob_free[t] = load(f"ob{t}", out[b * S + t * 128:b * S + (t + 1) * 128, :], ob[t][:], d_)
                    base_out.append(ob_free[0])
                    base_out.append(ob_free[1])
                    if b + 2 < B:
                        load_x(b + 2)
                after(1, store)

            load_values(0)
            load_values(1)
            after(8, lambda: load_x(0))
            after(9, lambda: load_stacks(2, 2))
            after(16, lambda: load_x(1))
            last = [None]

            def bc(ap, n):
                return ap.unsqueeze(2).to_broadcast([128, NT, n])

            def ch(fn, *w):
                last[0] = dve(fn, last[0], *w)
                return last[0]

            def tiles():
                last[0] = run_t[0]
                ch(lambda e: e.tensor_tensor(cn[:], run[:], EBASE, ALU.subtract))
                ch(lambda e: e.tensor_scalar(ci[:], cn[:], 255.0, None, ALU.add))
                ch(lambda e: e.tensor_scalar(cj[:], ci[:], 8, None, ALU.logical_shift_right))
                ch(lambda e: e.tensor_copy(nt[:], cj[:]))
                ch(lambda e: e.tensor_tensor_scan(en[:], onef[:, 0:NE], nt[:], 0.0, ALU.mult, ALU.add), t_onef)
                ch(lambda e: e.tensor_tensor(sn[:], en[:], nt[:], ALU.subtract))
                ch(lambda e: e.tensor_tensor(b8[:], TI8, en[:].unsqueeze(1).to_broadcast([128, NT, NE]), ALU.is_ge))
                ch(lambda e: e.tensor_reduce(Ei[:], b8[:], AX, ALU.add))
                ch(lambda e: e.tensor_tensor(ohE[:], IT8, bc(Ei[:], NE), ALU.is_equal))
                ch(lambda e: e.tensor_scalar(e0[:], Ei[:, 0:1], -float(NE), None, ALU.add))
                ch(lambda e: e.tensor_scalar(pd[:], Ei[:], float(NE), e0[:, 0:1], ALU.is_equal, ALU.mult))
                ch(lambda e: e.tensor_tensor(Ei[:], Ei[:], pd[:], ALU.add))
                ch(lambda e: e.tensor_tensor(ohE[:], IT8, bc(Ei[:], NE), ALU.is_equal))
                ch(lambda e: e.tensor_scalar(ba[:], Ei[:], 128.0, PIDX, ALU.mult, ALU.add))
                t_wx = ch(lambda e: e.tensor_copy(wx[:], ba[:]))
                ch(lambda e: e.tensor_scalar(gj[:], en[:], SPT, None, ALU.is_le))
                ch(lambda e: e.tensor_reduce(gk[:, 0:1], gj[:], AX, ALU.add))
                ch(lambda e: e.tensor_scalar(gj[:], IO8, gk[:, 0:1], None, ALU.is_equal))
                ch(lambda e: e.tensor_tensor(gj[:], gj[:], sn[:], ALU.mult))
                ch(lambda e: e.tensor_reduce(gk[:, 1:2], gj[:], AX, ALU.add))
                ch(lambda e: e.tensor_scalar(gk[:, 2:3], gk[:, 0:1], float(ER // 128), SPR, ALU.mult, ALU.add))
                ch(lambda e: e.scalar_tensor_tensor(out=gk[:, 3:4], in0=gk[:, 1:2], scalar=-2.0, in1=gk[:, 2:3],
                                                    op0=ALU.mult, op1=ALU.add))
                ch(lambda e: e.tensor_scalar(gk[:, 2:3], gk[:, 3:4], float(TR), None, ALU.min))
                t_gi = ch(lambda e: e.tensor_copy(gi[:], gk[:, 2:3]))
                return t_wx, t_gi

            meta = []
            placed = []

            def route(b):
                keep = {}

                def first():
                    keep["M"], keep["e"], keep["o"] = choose(b)

                def second():
                    keep["g"] = rank(b, keep["M"])
                    keep["y"], keep["z"] = weigh(b, keep["e"], keep["o"])

                def third():
                    place(b, keep["g"], keep["y"])
                    if b == B - 1:
                        placed.extend((dsem[k], dcount[k]) for k in ("sc0", "sc1", "hr0", "hr1"))
                        meta.extend(tiles())

                def fourth():
                    keep["a"] = turn_scores(b, keep["z"])

                for n, fn in ((0, lambda: out_project(b, 0)), (1, lambda: out_project(b, 1)),
                              (5, lambda: router_turn(b, 0)), (6, lambda: router_turn(b, 1)),
                              (7, lambda: router(b, 0)), (8, lambda: router(b, 1)), (9, first), (10, second),
                              (12, third), (13, fourth), (14, lambda: add_bias(b, keep["a"]))):
                    after(n, fn)

            for step in range(-1, B + 2):
                bB, bC, bD = step + 1, step, step - 1
                for n in range(9 if step < 0 else 0, NH):
                    if bD == B - 1 and n == 6:
                        after(1, lambda: route(B - 1))
                    if bD < B - 1 and n == 7 and bD >= 0:
                        after(1, lambda bD=bD: route(bD))
                    step_on()
                    if bB < B:
                        score_max(bB, n)
                        if n == 10:
                            send_max(bB, 0)
                    if 0 <= bC < B:
                        probs(bC, n)
                        if n == 2:
                            send_max(bC, 1)
                    if 0 <= bD < B and n == 1:
                        gv = values(bD, 3)
                        if bD + 3 < B:
                            st_free[bD % 3] = [gv]
                            load_stacks(bD + 3, 2)
                    if 0 <= bC < B and n >= 5 and n % 4 == 1:
                        values(bC, n // 4 - 1)
            assert not agenda
            over_b = [(done[n], count[n]) for n in ("tensor", "vector", "scalar", "gpsimd")] + placed
        wo_ctx.close()

        with ExitStack() as ctx:
            raw = [sb(ctx, f"raw{i}", [128, DW]) for i in range(3)]
            gb = [sb(ctx, f"gb{i}", [128, 8]) for i in range(2)]
            xs = [sb(ctx, f"xs{i}", [128, 2, RW]) for i in range(2)]
            wh = [sb(ctx, "eh0", [128, 3, GW], F32R)]
            wl = [sb(ctx, "el0", [128, 3, GW], F32R)]
            xh = [sb(ctx, f"xh{i}", [128, C, S], F32R) for i in range(2)]
            xl = [sb(ctx, f"xl{i}", [128, C, S], F32R) for i in range(2)]
            ga = [sb(ctx, f"ga{i}", [128, S]) for i in range(3)]
            up = [sb(ctx, f"up{i}", [128, S]) for i in range(3)]
            sg = [sb(ctx, f"sg{i}", [128, S]) for i in range(3)]
            ah = [sb(ctx, f"ah{i}", [128, C, S], F32R) for i in range(2)]
            al = [sb(ctx, f"al{i}", [128, C, S], F32R) for i in range(2)]
            ys = [sb(ctx, f"ys{i}", [128, D]) for i in range(2)]
            ww = [sb(ctx, f"ww{i}", [128, 2]) for i in range(3)]
            wh.append(sb(ctx, "eh1", [128, 3, GW], F32R))
            wl.append(sb(ctx, "el1", [128, 3, GW], F32R))
            pw = sb(ctx, "pw", [128, 2, NE])
            t_wx, t_gi = meta
            raw_free = [None] * 3
            wh_free = [[None] * 3, [None] * 3]
            gb_free = [None, None]
            xs_free = [[], []]
            xs_in = {}
            w_ok = {}

            def gather(key, dst, src, idx, *w):
                return dma("gpsimd", key, lambda e: e.indirect_dma_start(
                    dst, None, src, bass.IndirectOffsetOnAxis(ap=idx, axis=0)), *w)

            def fetch_x(i):
                for r in range(2):
                    z = gather(f"xs{i % 2}", xs[i % 2][:, r, :], hb, gx[:, 2 * i + r:2 * i + r + 1], t_gx, *xs_free[i % 2],
                               *(over_b if i < 2 else ()))
                xs_in[i] = z

            def fetch_w(i, part):
                src = (wga, wgb, wd)[part]
                n = DW if part == 1 else GW
                z = gather(f"raw{part}", raw[part][:, 0:n], src, wx[:, i:i + 1], t_wx, *(raw_free[part] or ()),
                           *([projected_o[0]] if i == 0 else ()))
                w_in[(i, part)] = z

            w_in = {}

            def split_high(i, part):
                p = i % 2
                th = act(lambda e: e.activation(wh[p][:, part, :], raw[part][:, 0:GW], ACT.Copy), w_in[(i, part)],
                         wh_free[p][part], *(over_b if i == 0 else base_out[-2:] if i == 1 else ()))
                w_hi[(i, part)] = th

            def split_low(i, part):
                p = i % 2
                th = w_hi[(i, part)]
                if part == 1:
                    tb = dve(lambda e: e.tensor_copy(gb[p][:], raw[1][:, GW:DW]), w_in[(i, 1)], *(gb_free[p] or over_b))
                tl = dve(lambda e: e.tensor_tensor(wl[p][:, part, :], raw[part][:, 0:GW], wh[p][:, part, :].bitcast(F32),
                                                   ALU.subtract), th)
                raw_free[part] = [th, tl]
                w_ok[(i, part)] = [th, tl] + ([tb] if part == 1 else [])
                if i + 1 < NT:
                    fetch_w(i + 1, part)

            w_hi = {}
            x_ok = {}
            xh_free = [None, None]
            ww_free = [None] * 3
            ww_t = {}

            def turn_x(i):
                p = i % 2
                for r in range(2):
                    k = 4 + r
                    g = pe(transposes(bank[k], xs[p][:, r, :], 4), xs_in[i], *free[k])
                    th, tl = split_psum(xh[p][:, :, r * 128:(r + 1) * 128], xl[p][:, :, r * 128:(r + 1) * 128],
                                        bank[k][:].rearrange("p (c n) -> p c n", c=4), g, xh_free[p])
                    free[k] = [th, tl]
                a_ = dve(lambda e: e.tensor_tensor(pw[:], xs[p][:, :, 512:520],
                                                   ohE[:, i, :].unsqueeze(1).to_broadcast([128, 2, NE]), ALU.mult), xs_in[i])
                ww_t[i] = dve(lambda e: e.tensor_reduce(ww[i % 3][:], pw[:], AX, ALU.add), a_, ww_free[i % 3])
                xs_free[p] = [g, a_]
                x_ok[i] = (th, tl)

            a_ok = {}
            a_free = [None, None]
            ga_free = [None] * 3
            up_free = [None] * 3
            sg_free = [None] * 3
            stage = {}

            def gate_up(i, m):
                p = i % 2
                n = C * i + m
                k = n % 4
                q = n % 3
                def emit(e):
                    for h in range(2):
                        o = bank[k][:, h * 256:(h + 1) * 256]
                        for c in range(C):
                            off = (c % 2) * 1024 + h * 512 + m * 128
                            lh = wh[p][:, c // 2, off:off + 128]
                            ll = wl[p][:, c // 2, off:off + 128]
                            nc.tensor.matmul(o, lh, xh[p][:, c, :], start=(c == 0), stop=False)
                            nc.tensor.matmul(o, lh, xl[p][:, c, :], start=False, stop=False)
                            last_ = nc.tensor.matmul(o, ll, xh[p][:, c, :], start=False, stop=(c == C - 1))
                    return last_
                g = pe(emit, *x_ok[i], *w_ok[(i, 0)], *w_ok[(i, 1)], *free[k])
                if m == C - 1:
                    xh_free[p] = g
                    wh_free[p][0] = wh_free[p][1] = g
                tb = w_ok[(i, 1)][2]
                g_ = dve(lambda e: e.tensor_scalar(ga[q][:], bank[k][:, 0:256], gb[p][:, m:m + 1], LIMIT, ALU.add, ALU.min),
                         g, tb, ga_free[q])
                u_ = act(lambda e: e.activation(up[q][:], bank[k][:, 256:512], ACT.Identity, bias=gb[p][:, 4 + m:5 + m]),
                         g_, up_free[q])
                s_ = act(lambda e: e.activation(sg[q][:], ga[q][:], ACT.Sigmoid, scale=ALPHA), g_, sg_free[q])
                free[k] = [u_, g_]
                gb_free[p] = (u_, g_)
                stage[n] = (g_, u_, s_)

            def activate(n):
                i, m = divmod(n, C)
                if not 0 <= i < NT:
                    return
                p = i % 2
                q = n % 3
                g_, u_, s_ = stage[n]
                v_ = dve(lambda e: e.tensor_scalar(up[q][:], up[q][:], LIMIT, -LIMIT, ALU.min, ALU.max), u_)
                y_ = dve(lambda e: e.scalar_tensor_tensor(out=up[q][:], in0=up[q][:], scalar=1.0, in1=ga[q][:],
                                                          op0=ALU.add, op1=ALU.mult), v_, g_)
                z_ = dve(lambda e: e.tensor_tensor(sg[q][:], up[q][:], sg[q][:], ALU.mult), y_, s_)
                h_ = act(lambda e: e.activation(ah[p][:, m, :], sg[q][:], ACT.Copy), z_, a_free[p])
                ga_free[q] = z_
                up_free[q] = z_
                stage[n] = h_

            def activate_low(n):
                i, m = divmod(n, C)
                if not 0 <= i < NT:
                    return
                p = i % 2
                q = n % 3
                h_ = stage[n]
                l_ = dve(lambda e: e.tensor_tensor(al[p][:, m, :], sg[q][:], ah[p][:, m, :].bitcast(F32), ALU.subtract), h_)
                sg_free[q] = l_
                a_ok[i] = (h_, l_)

            ys_free = [None, None]
            add_t = [None]

            def down(i, r):
                p = i % 2
                k = 6 + r
                lh = [ah[p][:, c, r * 128:(r + 1) * 128] for c in range(C)]
                ll = [al[p][:, c, r * 128:(r + 1) * 128] for c in range(C)]
                rh = [wh[p][:, 2, c * D:(c + 1) * D] for c in range(C)]
                rl = [wl[p][:, 2, c * D:(c + 1) * D] for c in range(C)]
                g = pe(mm3(bank[k][:], lh, ll, rh, rl), *a_ok[i], *w_ok[(i, 2)], *free[k])
                a_ = act(lambda e: e.activation(ys[r][:], bank[k][:], ACT.Copy, scale=ww[i % 3][:, r:r + 1]), g, ww_t[i], ys_free[r])
                free[k] = [a_]
                if r == 1:
                    wh_free[p][2] = g
                    a_free[p] = g
                    ww_free[i % 3] = a_
                return a_

            def add_rows(i, toks):
                p = i % 2
                prev = add_t[0]
                for r in range(2):
                    z = dma("gpsimd", f"add{p}", lambda e, r=r: e.indirect_dma_start(
                        out, bass.IndirectOffsetOnAxis(ap=ti[:, 2 * i + r:2 * i + r + 1], axis=0), ys[r][:], None,
                        bounds_check=T - 1, oob_is_err=False, compute_op=ALU.add), toks[r], t_ti, *(prev or base_out))
                for r in range(2):
                    ys_free[r] = z
                add_t[0] = [z]

            fetch_w(0, 0)
            t_tab = dma("gpsimd", "tab", lambda e: e.indirect_dma_start(
                tab[:], None, slot.rearrange("(a n) o -> a (n o)", n=128),
                bass.IndirectOffsetOnAxis(ap=gi[0:2 * NT, :], axis=0)), t_gi, *placed)
            fetch_w(0, 1)
            g_ids = pe(lambda e: nc.tensor.transpose(bank[0][:, 0:2 * NT], tab[:], ident[0:2 * NT, 0:2 * NT]), t_tab, *free[0])
            ch(lambda e: e.tensor_copy(ids[:], bank[0][:, 0:2 * NT]), g_ids)
            free[0] = [last[0]]
            t_ti = ch(lambda e: e.tensor_copy(ti[:], ids[:]))
            ch(lambda e: e.tensor_scalar(ids[:], ids[:], float(T - 1), None, ALU.min))
            t_gx = ch(lambda e: e.tensor_copy(gx[:], ids[:]))
            fetch_x(0)
            fetch_w(0, 2)
            fetch_x(1)
            for part in range(2):
                split_high(0, part)
                split_low(0, part)
            turn_x(0)
            for i in range(NT + 1):
                for m in range(C):
                    n = C * i + m
                    if i < NT:
                        if m in (1, 2) and i + 1 < NT:
                            split_high(i + 1, m - 1)
                        if m in (2, 3) and i + 1 < NT:
                            split_low(i + 1, m - 2)
                        if m == 3:
                            split_high(i, 2)
                            split_low(i, 2)
                        gate_up(i, m)
                    activate(n - 1)
                    activate_low(n - 2)
                    if m == 0 and i + 1 < NT:
                        turn_x(i + 1)
                        if i + 2 < NT:
                            fetch_x(i + 2)
                    if m == 2 and i > 0:
                        y0 = down(i - 1, 0)
                    if m == 3 and i > 0:
                        add_rows(i - 1, [y0, down(i - 1, 1)])
            queues["sync"].append((None, [add_t[0][0]] + base_out[-2:], None, 0))

        block = top.enter_context(nc.Block())

        def drive(name):
            def body(e):
                seen = {}
                for fn, waits, sem, n in queues[name]:
                    for s, v in waits:
                        if seen.get(id(s), 0) < v:
                            e.wait_ge(s, v)
                            seen[id(s)] = v
                    if fn is not None:
                        fn(e).then_inc(sem, n)
            return body

        block.tensor(drive("tensor"))
        block.vector(drive("vector"))
        block.scalar(drive("scalar"))
        block.gpsimd(drive("gpsimd"))
        block.sync(drive("sync"))


def constants():
    p = np.arange(128)
    cst = np.zeros((2, 128, 128), np.float32)
    cst[0] = np.eye(128)
    cst[1] = p[:, None] < p[None, :]
    cm = np.zeros((128, 520), np.float32)
    cm[:, 0:32] = np.tile(np.arange(8), 4)
    cm[:, 32:40] = np.arange(8) * ER
    cm[:, 56] = p
    cm[:, 57] = (p < 8) | (p >= 16)
    cm[:, 58] = (p >= 8) & (p < 16)
    cm[:, 60] = p // 2
    cm[:, 61] = p
    i = np.arange(NT)
    cm[:, 136:136 + 8 * NT] = np.repeat(i, 8)
    cm[:, 320:320 + 8 * NT] = np.tile(np.arange(8), NT)
    cm[:, 504:520] = p[:, None] + 128 * np.arange(16)[None, :]
    return cst, cm


def kernel(**inputs):
    import concourse.bacc as _bacc
    from concourse import mybir as _mybir
    from concourse.bass_utils import run_bass_kernel_spmd as _run

    g = {k: np.asarray(v) for k, v in inputs.items()}
    a = "L0_xattn_"
    f = "L0_ffn_"
    cst, cm = constants()
    cm[:, 40:56] = np.tile(g[f + "router_bias"], 2)[None, :]
    gu = g[f + "gate_up_proj"].reshape(NE, C, 128, C, 128, 2).transpose(0, 2, 1, 5, 3, 4).reshape(NE * 128, C, 1024)
    dn = g[f + "down_proj"].reshape(NE, C, 128, D).transpose(0, 2, 1, 3).reshape(NE * 128, C * D)
    gbias = g[f + "gate_up_proj_bias"].reshape(NE, C, 128, 2).transpose(0, 2, 3, 1).reshape(NE * 128, 8)
    arrays = {
        "in_x": g["x"].reshape(T, D),
        "in_ctxT": g["ctx_2048"].transpose(0, 2, 1).reshape(B, C, 128, S).transpose(0, 2, 1, 3).reshape(B, 128, C * S),
        "in_w": np.stack([g[a + n].T.reshape(C, 128, D).transpose(1, 0, 2).reshape(128, C * D)
                          for n in ("w_q", "w_k_img", "w_v_img", "w_o")]),
        "in_bias": np.stack([np.broadcast_to(g[a + n], (128, D))
                             for n in ("b_q", "b_k_img", "b_v_img", "g_q", "g_k_img", "b_o")]),
        "in_bd3": np.concatenate([g[f + "down_proj_bias"]] * 3),
        "in_rwT": g[f + "router_weight"].T.reshape(C, 128, NE).transpose(1, 0, 2).reshape(128, C * NE),
        "in_wga": gu[:, 0:2].reshape(NE * 128, GW),
        "in_wgb": np.concatenate([gu[:, 2:4].reshape(NE * 128, GW), gbias], axis=1),
        "in_wd": dn,
        "in_cst": cst,
        "in_cm": cm,
    }
    arrays = {k: np.ascontiguousarray(v) for k, v in arrays.items()}
    nc = _bacc.Bacc("TRN2", target_bir_lowering=False, num_devices=1)
    args = [nc.dram_tensor(k, v.shape, _mybir.dt.from_np(v.dtype), kind="ExternalInput").ap() for k, v in arrays.items()]
    args.append(nc.dram_tensor("out_0", (T, D), _mybir.dt.float32, kind="ExternalOutput").ap())
    program(nc, *args)
    r = _run(nc, [arrays], core_ids=[0])
    return r.results[0]["out_0"].reshape(B, S, D)
```
